# Optimizing a Trainium2 kernel written in Bass

```python
import numpy as np
import jax
import jax.numpy as jnp

def _softmax(x, axis=-1):
    return jax.nn.softmax(x, axis=axis)

def _gelu(x):
    return jax.nn.gelu(x, approximate=True)

def _silu(x):
    return jax.nn.silu(x)

def _sigmoid(x):
    return jax.nn.sigmoid(x)

def _layernorm(x, axis=-1, eps=1e-05):
    m = jnp.mean(x, axis=axis, keepdims=True)
    v = jnp.var(x, axis=axis, keepdims=True)
    return (x - m) / jnp.sqrt(v + eps)

def _scatter_add(tgt, idx, src, axis=0):
    return tgt.at[idx].add(src)

def _segment_sum(src, seg, n):
    return jax.ops.segment_sum(src, seg, n)
kernel_name = 'mk_rec_standalone_d1_rec_r8_401c7f'

def setup_inputs(seed: int=0):
    np.random.seed(seed)
    _w = jnp.asarray

    def _rec_inputs():
        import jax
        import jax.numpy as jnp
        _rk = jax.random.key(seed)
        r_numerical_input = -0.00338568 + 1.0005 * jax.random.normal(jax.random.fold_in(_rk, 1), (2048, 13), jnp.float32)
        r_categorical_inputs = jnp.stack([jax.random.randint(jax.random.fold_in(jax.random.fold_in(_rk, 2), 0), (2048,), 2, 12500, jnp.int32), jax.random.randint(jax.random.fold_in(jax.random.fold_in(_rk, 2), 1), (2048,), 1, 99999, jnp.int32), jax.random.randint(jax.random.fold_in(jax.random.fold_in(_rk, 2), 2), (2048,), 0, 12500, jnp.int32), jax.random.randint(jax.random.fold_in(jax.random.fold_in(_rk, 2), 3), (2048,), 5, 12500, jnp.int32), jax.random.randint(jax.random.fold_in(jax.random.fold_in(_rk, 2), 4), (2048,), 20, 99993, jnp.int32), jax.random.randint(jax.random.fold_in(jax.random.fold_in(_rk, 2), 5), (2048,), 0, 99993, jnp.int32), jax.random.randint(jax.random.fold_in(jax.random.fold_in(_rk, 2), 6), (2048,), 2, 99999, jnp.int32), jax.random.randint(jax.random.fold_in(jax.random.fold_in(_rk, 2), 7), (2048,), 2, 99995, jnp.int32), jax.random.randint(jax.random.fold_in(jax.random.fold_in(_rk, 2), 8), (2048,), 0, 99999, jnp.int32), jax.random.randint(jax.random.fold_in(jax.random.fold_in(_rk, 2), 9), (2048,), 2, 99986, jnp.int32), jax.random.randint(jax.random.fold_in(jax.random.fold_in(_rk, 2), 10), (2048,), 4, 99999, jnp.int32), jax.random.randint(jax.random.fold_in(jax.random.fold_in(_rk, 2), 11), (2048,), 15, 99999, jnp.int32), jax.random.randint(jax.random.fold_in(jax.random.fold_in(_rk, 2), 12), (2048,), 0, 99989, jnp.int32), jax.random.randint(jax.random.fold_in(jax.random.fold_in(_rk, 2), 13), (2048,), 5, 99990, jnp.int32), jax.random.randint(jax.random.fold_in(jax.random.fold_in(_rk, 2), 14), (2048,), 2, 99996, jnp.int32), jax.random.randint(jax.random.fold_in(jax.random.fold_in(_rk, 2), 15), (2048,), 3, 99994, jnp.int32), jax.random.randint(jax.random.fold_in(jax.random.fold_in(_rk, 2), 16), (2048,), 0, 99998, jnp.int32), jax.random.randint(jax.random.fold_in(jax.random.fold_in(_rk, 2), 17), (2048,), 13, 99998, jnp.int32), jax.random.randint(jax.random.fold_in(jax.random.fold_in(_rk, 2), 18), (2048,), 10, 12498, jnp.int32), jax.random.randint(jax.random.fold_in(jax.random.fold_in(_rk, 2), 19), (2048,), 0, 99999, jnp.int32), jax.random.randint(jax.random.fold_in(jax.random.fold_in(_rk, 2), 20), (2048,), 0, 99995, jnp.int32), jax.random.randint(jax.random.fold_in(jax.random.fold_in(_rk, 2), 21), (2048,), 1, 99998, jnp.int32), jax.random.randint(jax.random.fold_in(jax.random.fold_in(_rk, 2), 22), (2048,), 1, 99997, jnp.int32), jax.random.randint(jax.random.fold_in(jax.random.fold_in(_rk, 2), 23), (2048,), 2, 99989, jnp.int32), jax.random.randint(jax.random.fold_in(jax.random.fold_in(_rk, 2), 24), (2048,), 6, 12500, jnp.int32), jax.random.randint(jax.random.fold_in(jax.random.fold_in(_rk, 2), 25), (2048,), 2, 99995, jnp.int32)], axis=1)
        return (r_numerical_input, r_categorical_inputs)
    r_numerical_input, r_categorical_inputs = _rec_inputs()

    def _L0_rec_setup():
        import jax, jax.numpy as jnp
        import numpy as np
        B = 2048
        NUM_DENSE = 13
        NUM_TABLES = 26
        VOCAB = 12500
        D = 128
        BOT = [512, 256, 128]
        TOP = [1024, 1024, 512, 256, 1]
        TOP_IN = 27 * 26 // 2 + D + 1

        def _linear_params(key, fan_in, fan_out):
            kw, kb = jax.random.split(key)
            w = jax.random.normal(kw, (fan_out, fan_in), jnp.float32) * np.sqrt(2.0 / (fan_in + fan_out))
            b = jax.random.normal(kb, (fan_out,), jnp.float32) * np.sqrt(1.0 / fan_out)
            return (w, b)

        def _dlrm_forward(numerical_input, categorical_inputs, emb_tables, bot_params, top_params):
            x = numerical_input
            for w, b in bot_params:
                x = jax.nn.relu(x @ w.T + b)
            bottom = x
            emb = jax.vmap(lambda tbl, idx: tbl[idx])(emb_tables, categorical_inputs.T)
            concat = jnp.concatenate([bottom[:, None, :], jnp.transpose(emb, (1, 0, 2))], axis=1)
            inter = jnp.einsum('bnd,bmd->bnm', concat, concat)
            ti, tj = jnp.tril_indices(NUM_TABLES + 1, -1)
            inter_flat = inter[:, ti, tj]
            pad = jnp.zeros((numerical_input.shape[0], 1), dtype=bottom.dtype)
            y = jnp.concatenate([bottom, inter_flat, pad], axis=1)
            for w, b in top_params[:-1]:
                y = jax.nn.relu(y @ w.T + b)
            w, b = top_params[-1]
            return y @ w.T + b
        key = jax.random.key(seed)
        ks = jax.random.split(key, 16)
        numerical_input = jax.random.normal(ks[0], (B, NUM_DENSE), jnp.float32)
        categorical_inputs = jax.random.randint(ks[1], (B, NUM_TABLES), 0, VOCAB, jnp.int64 if jax.config.jax_enable_x64 else jnp.int32)
        bound = np.sqrt(1.0 / VOCAB)
        emb_tables = jax.random.uniform(ks[2], (NUM_TABLES, VOCAB, D), jnp.float32, -bound, bound)
        bw0, bb0 = _linear_params(ks[3], NUM_DENSE, BOT[0])
        bw1, bb1 = _linear_params(ks[4], BOT[0], BOT[1])
        bw2, bb2 = _linear_params(ks[5], BOT[1], BOT[2])
        tw0, tb0 = _linear_params(ks[6], TOP_IN, TOP[0])
        tw0 = tw0.at[:, -1].set(0.0)
        tw1, tb1 = _linear_params(ks[7], TOP[0], TOP[1])
        tw2, tb2 = _linear_params(ks[8], TOP[1], TOP[2])
        tw3, tb3 = _linear_params(ks[9], TOP[2], TOP[3])
        tw4, tb4 = _linear_params(ks[10], TOP[3], TOP[4])
        return dict(numerical_input=numerical_input, categorical_inputs=categorical_inputs, emb_tables=emb_tables, bw0=bw0, bb0=bb0, bw1=bw1, bb1=bb1, bw2=bw2, bb2=bb2, tw0=tw0, tb0=tb0, tw1=tw1, tb1=tb1, tw2=tw2, tb2=tb2, tw3=tw3, tb3=tb3, tw4=tw4, tb4=tb4)
    _L0_rec_all = _L0_rec_setup()
    _L0_rec_in = {k: v for k, v in _L0_rec_all.items() if k in ('emb_tables', 'bw0', 'bb0', 'bw1', 'bb1', 'bw2', 'bb2', 'tw0', 'tb0', 'tw1', 'tb1', 'tw2', 'tb2', 'tw3', 'tb3', 'tw4', 'tb4')}
    del _L0_rec_all
    return {'r_numerical_input': r_numerical_input, 'r_categorical_inputs': r_categorical_inputs, 'L0_rec_emb_tables': _L0_rec_in['emb_tables'], 'L0_rec_bw0': _L0_rec_in['bw0'], 'L0_rec_bb0': _L0_rec_in['bb0'], 'L0_rec_bw1': _L0_rec_in['bw1'], 'L0_rec_bb1': _L0_rec_in['bb1'], 'L0_rec_bw2': _L0_rec_in['bw2'], 'L0_rec_bb2': _L0_rec_in['bb2'], 'L0_rec_tw0': _L0_rec_in['tw0'], 'L0_rec_tb0': _L0_rec_in['tb0'], 'L0_rec_tw1': _L0_rec_in['tw1'], 'L0_rec_tb1': _L0_rec_in['tb1'], 'L0_rec_tw2': _L0_rec_in['tw2'], 'L0_rec_tb2': _L0_rec_in['tb2'], 'L0_rec_tw3': _L0_rec_in['tw3'], 'L0_rec_tb3': _L0_rec_in['tb3'], 'L0_rec_tw4': _L0_rec_in['tw4'], 'L0_rec_tb4': _L0_rec_in['tb4']}

def reference(r_numerical_input, r_categorical_inputs, L0_rec_emb_tables, L0_rec_bw0, L0_rec_bb0, L0_rec_bw1, L0_rec_bb1, L0_rec_bw2, L0_rec_bb2, L0_rec_tw0, L0_rec_tb0, L0_rec_tw1, L0_rec_tb1, L0_rec_tw2, L0_rec_tb2, L0_rec_tw3, L0_rec_tb3, L0_rec_tw4, L0_rec_tb4):
    import jax
    import jax.numpy as jnp

    def _L0_rec_ref(numerical_input, categorical_inputs, emb_tables, bw0, bb0, bw1, bb1, bw2, bb2, tw0, tb0, tw1, tb1, tw2, tb2, tw3, tb3, tw4, tb4):
        import jax, jax.numpy as jnp
        import numpy as np
        B = 2048
        NUM_DENSE = 13
        NUM_TABLES = 26
        VOCAB = 12500
        D = 128
        BOT = [512, 256, 128]
        TOP = [1024, 1024, 512, 256, 1]
        TOP_IN = 27 * 26 // 2 + D + 1

        def _linear_params(key, fan_in, fan_out):
            kw, kb = jax.random.split(key)
            w = jax.random.normal(kw, (fan_out, fan_in), jnp.float32) * np.sqrt(2.0 / (fan_in + fan_out))
            b = jax.random.normal(kb, (fan_out,), jnp.float32) * np.sqrt(1.0 / fan_out)
            return (w, b)

        def _dlrm_forward(numerical_input, categorical_inputs, emb_tables, bot_params, top_params):
            x = numerical_input
            for w, b in bot_params:
                x = jax.nn.relu(x @ w.T + b)
            bottom = x
            emb = jax.vmap(lambda tbl, idx: tbl[idx])(emb_tables, categorical_inputs.T)
            concat = jnp.concatenate([bottom[:, None, :], jnp.transpose(emb, (1, 0, 2))], axis=1)
            inter = jnp.einsum('bnd,bmd->bnm', concat, concat)
            ti, tj = jnp.tril_indices(NUM_TABLES + 1, -1)
            inter_flat = inter[:, ti, tj]
            pad = jnp.zeros((numerical_input.shape[0], 1), dtype=bottom.dtype)
            y = jnp.concatenate([bottom, inter_flat, pad], axis=1)
            for w, b in top_params[:-1]:
                y = jax.nn.relu(y @ w.T + b)
            w, b = top_params[-1]
            return y @ w.T + b
        bot = [(bw0, bb0), (bw1, bb1), (bw2, bb2)]
        top = [(tw0, tb0), (tw1, tb1), (tw2, tb2), (tw3, tb3), (tw4, tb4)]
        return _dlrm_forward(numerical_input, categorical_inputs, emb_tables, bot, top)
    y = _L0_rec_ref(r_numerical_input, r_categorical_inputs, L0_rec_emb_tables, L0_rec_bw0, L0_rec_bb0, L0_rec_bw1, L0_rec_bb1, L0_rec_bw2, L0_rec_bb2, L0_rec_tw0, L0_rec_tb0, L0_rec_tw1, L0_rec_tb1, L0_rec_tw2, L0_rec_tb2, L0_rec_tw3, L0_rec_tb3, L0_rec_tw4, L0_rec_tb4)
    return y

_drawn_inputs = setup_inputs


def setup_inputs(seed=0):
    import zlib

    import numpy as np

    out = dict(_drawn_inputs(seed))
    spreads = {}
    factors = {}
    for name, (base, spread) in spreads.items():
        noise = np.random.default_rng([zlib.crc32(name.encode()), seed]).standard_normal(out[name].shape)
        drawn = base * np.exp(spread * noise) if base else spread * noise
        out[name] = jnp.asarray(drawn.astype(out[name].dtype))
    for name, factor in factors.items():
        out[name] = (out[name] * factor).astype(out[name].dtype)
    return out
```

```python
from contextlib import ExitStack

import concourse.bass as bass
from concourse import mybir

ALU = mybir.AluOpType
ACT = mybir.ActivationFunctionType
F32 = mybir.dt.float32
F32R = mybir.dt.float32r
I32 = mybir.dt.int32

P = 128
BATCH = 2048
TILE = 512
TILES = BATCH // TILE
UNITS = TILE // P
TABLES = 26
VOCAB = 12500
D = 128
ITEMS = TABLES + 1
ITEM_PITCH = 32
PAIRS = ITEMS * (ITEMS - 1) // 2
TOP_IN = D + PAIRS + 1
DENSE = 13
S = 4
GRAM_M = (S - 1) * ITEM_PITCH + ITEMS
COLS = ITEMS - 1

CHUNK = 4
CHUNKS = -(-TABLES // CHUNK)
WIDTH = [min(CHUNK, TABLES - CHUNK * k) for k in range(CHUNKS)]
GRAMS = 4
FWDS = -(-COLS // CHUNK)
PAIR_TILES = 3
PAIR_ROWS = [P, P, PAIRS + 1 - 2 * P]

TP_FWD = UNITS * CHUNKS
TP_BACK = TP_FWD + FWDS
TP_USES = TP_BACK + PAIR_TILES
GP_USES = UNITS * GRAMS

BOT_SIZES = [512, 256, 128]
BOT_BLOCKS = 7
NB = TILES * BOT_BLOCKS
BOT_SPLIT = 6
L0, L1, L2, L3, L4 = 0, 8, 16, 20, 22
BLOCKS = 24
SPLIT_BLOCKS = 22
STREAM = 12
RAW_HEAD = 10
RAWC = 1024

TP_ENGINE = ["D" if c % 3 == 2 else "A" for c in range(TP_FWD)] + ["D"] * FWDS + ["B"] * PAIR_TILES


def used(engine, r):
    return sum(e in (engine, "B") for e in TP_ENGINE[:r + 1])


TPA, TPD = used("A", TP_USES), used("D", TP_USES)


def pair_at(n):
    return sum(ITEMS - 1 - i for i in range(n))


def front_steps():
    steps = []
    for u in range(UNITS):
        for k in range(CHUNKS):
            steps.append(("chunk", CHUNKS * u + k))
            if u and k in (1, 2, 4, 5):
                steps.append(("gram", GRAMS * (u - 1) + [1, 2, 4, 5].index(k)))
    return steps + [("gram", GRAMS * (UNITS - 1) + h) for h in range(GRAMS)]


def head_schedule():
    def bottoms(a):
        return [("bottom", t, b) for b in range(BOT_BLOCKS) for t in (a, a + 1)]

    steps = [("raw", r) for r in range(4)] + bottoms(0) + [("raw", 4)]
    front = front_steps()
    late = bottoms(2)
    for i, b in enumerate(late):
        if i % 2 == 0:
            steps.append(front.pop(0))
        steps.append(b)
        if i in (2, 4, 6, 8, 10):
            steps.append(("raw", 5 + (i - 2) // 2))
    steps += [("split", 0), ("split", 1)] + front
    steps += [("fwd", f) for f in range(FWDS)] + [("back", k) for k in range(PAIR_TILES)]
    return steps + [("x0",)]


def body_schedule(with_front):
    cost = [1] * 8 + [2] * 12
    front = front_steps() if with_front else []
    lead, spread = 3, 19.0
    steps, total = [], sum(cost[:19])
    done, put, whole = 0, 0, len(front)

    def feed(upto):
        nonlocal put
        while put < upto and front:
            steps.append(front.pop(0))
            put += 1

    feed(lead)
    for b in range(20):
        if b == 18:
            feed(whole)
        steps.append(("block", b))
        if L1 <= b < L3 and (with_front or b - L1 < STREAM - 2):
            steps.append(("split", b - L1 + 2))
        done += cost[b]
        feed(lead + int((whole - lead) * done / (total - 2)))
        if with_front and b == 18:
            steps += [("fwd", f) for f in range(4)]
    if with_front:
        steps += [("fwd", f) for f in range(4, FWDS)]
    steps += [("block", 20), ("block", 21)]
    if with_front:
        steps += [("back", k) for k in range(PAIR_TILES)] + [("x0",)]
    return steps + [("block", 22), ("block", 23)]


def dlrm(nc, idx, xt, bw0, bw1, bw2, bias, w4, b4, wt0, wt3, wstream, tables, y):
    head, body, tail = head_schedule(), body_schedule(True), body_schedule(False)
    with ExitStack() as ctx:
        def sb(name, shape, dt):
            return ctx.enter_context(nc.sbuf_tensor(name, shape, dt))

        def sem(name):
            return ctx.enter_context(nc.semaphore(name))

        W0 = sb("W0", [P, 2, 4, 1024], F32R)
        W3 = sb("W3", [P, 2, RAWC], F32R)
        W4 = sb("W4", [P, 2, 2], F32R)
        Wring = sb("Wring", [P, 2, 2, RAWC], F32R)
        raw = sb("raw", [P, 2, RAWC], F32)
        w4raw = sb("w4raw", [P, 2], F32)
        A = sb("A", [P, 16, TILE], F32R)
        B = sb("B", [P, 16, TILE], F32R)
        staged = sb("staged", [P, 2, TILE], F32)
        bottom_out = sb("bottom_out", [P, BATCH], F32)
        biases = sb("biases", [P, 29], F32)
        bias4 = sb("bias4", [1, 1], F32)
        G = sb("G", [P, TABLES * D], F32)
        E = sb("E", [P, 2, P, ITEM_PITCH], F32)
        X = sb("X", [P, COLS, P], F32)
        Z = sb("Z", [P, S, PAIRS + 1], F32)
        ident = sb("ident", [P, P], F32)
        idx_all = sb("idx_all", [P, TILES * UNITS * TABLES], I32)
        idx_unit = sb("idx_unit", [P, 2, TABLES], I32)

        tp = ctx.enter_context(nc.psum_tensor("tp", [P, 2, 512], F32))
        gp = ctx.enter_context(nc.psum_tensor("gp", [P, 2, 2, 512], F32))
        mp = ctx.enter_context(nc.psum_tensor("mp", [P, 2, 512], F32))

        XS = B[:, 8:12, :].rearrange("p a b -> p (a b)")
        BW0 = B[:, 12, :]

        idx_landed = sem("idx_landed")
        small_landed = sem("small_landed")
        raw_landed = [sem(f"raw_landed{i}") for i in range(2)]
        table_offsets = sem("table_offsets")
        consts = sem("consts")
        pads, e_pads = sem("pads"), sem("e_pads")
        idx_step = sem("idx_step")
        idx_ready = sem("idx_ready")
        idx_copied = sem("idx_copied")
        gather_turn = sem("gather_turn")
        gathered = [sem(f"gathered{k}") for k in range(CHUNKS)]
        w_hi, w_lo, w4_ready = sem("w_hi"), sem("w_lo"), sem("w4_ready")
        w4_hi = sem("w4_hi")
        tp_done, tp_act, tp_dve = sem("tp_done"), sem("tp_act"), sem("tp_dve")
        item0 = sem("item0")
        gp_done, gp_act, gp_dve = sem("gp_done"), sem("gp_act"), sem("gp_dve")
        x0_hi, x0_lo = sem("x0_hi"), sem("x0_lo")
        block_done = sem("block_done")
        block_emptied, h_lo = sem("block_emptied"), sem("h_lo")
        y_stored = sem("y_stored")

        block = ctx.enter_context(nc.Block())

        def bottom_number(t, b):
            return (t // 2) * 2 * BOT_BLOCKS + 2 * b + t % 2

        def bottom_splits(n):
            full, rest = divmod(n + 1, 2 * BOT_BLOCKS)
            return full * 2 * BOT_SPLIT + min(rest, 2 * BOT_SPLIT)

        def top_splits(T, b):
            return TILES * BOT_SPLIT + SPLIT_BLOCKS * T + b + 1

        def raw_number(T, k):
            return RAW_HEAD + STREAM * T + k

        @block.sync
        def _(sp):
            sp.dma_start(idx_all[:], idx).then_inc(idx_landed, 16)
            loads = [(raw[0:96, 0, 0:512], bw0), (raw[0:96, 1, :], xt[0]),
                     (raw[:, 0, :], bw1), (raw[:, 1, 0:256], bw2), (raw[0:96, 0, :], xt[1])]
            loads += [(raw[:, (5 + k) % 2, :], wt0[:, k, :]) for k in range(4)]
            loads += [(raw[:, 1, :], wt3)]
            for r, (dst, src) in enumerate(loads):
                if r >= 2:
                    sp.wait_ge(w_lo, r - 1)
                sp.dma_start(dst, src).then_inc(raw_landed[r % 2], 16)
                if r == 1:
                    sp.dma_start(biases[:], bias).then_inc(small_landed, 16)
                    sp.dma_start(w4raw[:], w4).then_inc(small_landed, 16)
                    sp.dma_start(bias4[:], b4).then_inc(small_landed, 16)
            for k in range(2):
                sp.wait_ge(w_lo, raw_number(0, k) - 1)
                sp.dma_start(raw[:, k, :], wstream[k]).then_inc(raw_landed[k], 16)

            def reload(T, k):
                sp.wait_ge(w_lo, raw_number(T, k) + 1)
                sp.dma_start(raw[:, k % 2, :], wstream[(k + 2) % STREAM]).then_inc(raw_landed[k % 2], 16)

            with sp.Fori(0, TILES - 1) as T:
                for k in range(STREAM):
                    reload(T, k)
            for k in range(STREAM - 2):
                reload(TILES - 1, k)
            sp.wait_ge(block_emptied, NB + BLOCKS * TILES)
            sp.dma_start(y, bottom_out[0:1, :]).then_inc(y_stored, 16)
            sp.wait_ge(y_stored, 16)

        @block.gpsimd
        def _(pool):
            offs = X[:, 0:4, :].rearrange("p a b -> p (a b)").bitcast(I32)[:, 0:TILES * UNITS * TABLES]
            pool.iota(offs.rearrange("p (a t) -> p a t", t=TABLES), pattern=[[0, TILES * UNITS], [VOCAB, TABLES]],
                      base=0, channel_multiplier=0).then_inc(table_offsets, 1)
            pool.memset(ident[:], 0.0).then_inc(consts, 1)
            pool.wait_ge(consts, 1)
            pool.affine_select(out=ident[:], in_=ident[:], compare_op=ALU.not_equal, fill=1.0, base=0,
                               pattern=[[-1, P]], channel_multiplier=1).then_inc(consts, 1)
            pool.wait_ge(idx_ready, 1)

            def copy_indices(U, par):
                pool.tensor_copy(idx_unit[:, par, :], idx_all[:, bass.ds(U * TABLES, TABLES)]).then_inc(idx_copied, 1)
                pool.wait_ge(idx_copied, U + 1)
                pool.sem_inc(gather_turn, 1)

            def gather_unit(T, u):
                U = UNITS * T + u
                for k in range(CHUNKS):
                    if u > 0:
                        pool.wait_ge(tp_done, TP_USES * T + CHUNKS * (u - 1) + k + 1)
                    if k == 0:
                        copy_indices(U, u % 2)
                    else:
                        pool.sem_inc(gather_turn, 1)
                    for i in range(WIDTH[k]):
                        t = CHUNK * k + i
                        pool.indirect_dma_start(G[:, t * D:(t + 1) * D], None, tables,
                                                bass.IndirectOffsetOnAxis(idx_unit[:, u % 2, t:t + 1], 0)
                                                ).then_inc(gathered[k], 16)

            gather_unit(0, 0)
            pool.memset(E[:, :, :, ITEMS:ITEM_PITCH], 0.0).then_inc(e_pads, 1)
            with pool.Fori(0, TILES - 1) as T:
                for u in range(1, UNITS + 1):
                    gather_unit(T, u)
            for u in range(1, UNITS):
                gather_unit(TILES - 1, u)

        def item0_source(T, j):
            tile = bottom_out[:, bass.ds(T * TILE, TILE)]
            return tile.rearrange("d (s j g) -> d j g s", s=S, j=UNITS)[:, j]

        def gram_copy(s, r):
            rows = ITEM_PITCH if s < S - 1 else ITEMS
            j, h = divmod(r, GRAMS)
            src = gp[32 * s:32 * s + rows, r % 2, :, 0:4 * S * COLS]
            src = src.rearrange("p b (i c) -> p b i c", c=S * COLS)[:, :, :, s * COLS:(s + 1) * COLS]
            dst = X[32 * s:32 * s + rows, :, 32 * j + 8 * h:32 * j + 8 * h + 8]
            return dst.rearrange("p n (b i) -> p b i n", b=2), src

        def chunk_copy(c):
            u, k = divmod(c, CHUNKS)
            dst = E[:, u % 2, :, 1 + CHUNK * k:1 + CHUNK * k + WIDTH[k]].rearrange("d p i -> d i p")
            return dst, tp[:, c % 2, 0:WIDTH[k] * P].rearrange("d (i p) -> d i p", i=WIDTH[k])

        def out_tiles(b):
            if b < L1:
                return A[:, b], A[:, 8 + b], 7 + b
            if b < L2:
                return B[:, b - L1], B[:, 8 + b - L1], 7 + b
            if b < L3:
                return A[:, b - L2], A[:, 4 + b - L2], 7 + b
            return B[:, 8 + b - L3], B[:, 10 + b - L3], 7 + b

        def bottom_tiles(t, b):
            if b < 4:
                return A[:, 8 * (t % 2) + b], A[:, 8 * (t % 2) + 4 + b], b
            return B[:, 4 * (t % 2) + b - 4], B[:, 4 * (t % 2) + b - 2], b

        def raw_parts(r):
            if r == 0:
                return raw[0:96, 0, 0:512], BW0[0:96], BW0, (32, 64)
            if r in (1, 4):
                half = XS[:, RAWC * (r // 4):RAWC * (r // 4 + 1)]
                return raw[0:96, r % 2, :], half[0:96], half, (64, 96)
            if r == 2:
                return raw[:, 0, :], Wring[:, 0, 0, :], Wring[:, 0, 1, :], (0, P)
            if r == 3:
                return raw[:, 1, 0:256], Wring[:, 1, 0, 0:256], Wring[:, 1, 1, 0:256], (0, P)
            if r < 9:
                return raw[:, r % 2, :], W0[:, 0, r - 5], W0[:, 1, r - 5], (0, P)
            return raw[:, 1, :], W3[:, 0], W3[:, 1], (0, P)

        def split_free(T, k):
            if isinstance(T, int) and T == 0 and k < 2:
                return NB
            return NB + BLOCKS * T + (L1 + k - 2 if k >= 2 else L1 + k - 2 + STREAM - BLOCKS) + 1

        @block.scalar
        def _(act):
            def relu_hi(hi, bank, col, done, n_split, par):
                act.wait_ge(block_done, done)
                act.activation(hi, mp[:, bank, :], ACT.Relu, bias=biases[:, col:col + 1])
                if not isinstance(n_split, int) or n_split > 2:
                    act.wait_ge(h_lo, n_split - 2)
                act.activation(staged[:, par], mp[:, bank, :], ACT.Relu, bias=biases[:, col:col + 1]
                               ).then_inc(block_emptied, 1)

            def step(kind, T, TF, *a):
                if kind == "raw":
                    r, = a
                    act.wait_ge(raw_landed[r % 2], 16 * (r // 2 + 1))
                    src, hi, _, _ = raw_parts(r)
                    act.activation(hi, src, ACT.Copy).then_inc(w_hi, 1)
                    if r == 3:
                        act.activation(W4[:, 0], w4raw[:], ACT.Copy).then_inc(w4_hi, 1)
                elif kind == "split":
                    k = a[0] % STREAM
                    TW = T if a[0] < STREAM else T + 1
                    act.wait_ge(raw_landed[k % 2], 16 * ((RAW_HEAD + k) // 2 + STREAM // 2 * TW + 1))
                    act.wait_ge(block_done, split_free(TW, k))
                    act.activation(Wring[:, k % 2, 0], raw[:, k % 2], ACT.Copy).then_inc(w_hi, 1)
                elif kind == "bottom":
                    t, b = a
                    n = bottom_number(t, b)
                    if b < BOT_SPLIT:
                        hi, _, col = bottom_tiles(t, b)
                        relu_hi(hi, n % 2, col, n + 1, bottom_splits(n), (bottom_splits(n) - 1) % 2)
                    else:
                        act.wait_ge(block_done, n + 1)
                        act.activation(bottom_out[:, t * TILE:(t + 1) * TILE], mp[:, n % 2, :], ACT.Relu,
                                       bias=biases[:, 6:7]).then_inc(block_emptied, 1)
                elif kind == "block":
                    b, = a
                    if b < L4:
                        hi, _, col = out_tiles(b)
                        relu_hi(hi, b % 2, col, NB + BLOCKS * T + b + 1, top_splits(T, b), b % 2)
                    else:
                        act.wait_ge(block_done, NB + BLOCKS * T + b + 1)
                        act.activation(bottom_out[0:1, bass.ds(T * TILE + (b - L4) * 256, 256)],
                                       mp[0:1, b % 2, 0:256], ACT.Identity, bias=bias4[:]).then_inc(block_emptied, 1)
                elif kind == "chunk":
                    c, = a
                    u, k = divmod(c, CHUNKS)
                    if k == 0:
                        act.wait_ge(tp_done, TP_USES * TF + c + 1)
                        act.wait_ge(block_emptied, 13 if isinstance(TF, int) else NB)
                        act.activation(E[:, u % 2, :, 0].rearrange("d (g s) -> d g s", s=S),
                                       item0_source(TF, u), ACT.Copy).then_inc(item0, 1)
                    if TP_ENGINE[c] == "A":
                        act.wait_ge(tp_done, TP_USES * TF + c + 1)
                        dst, src = chunk_copy(c)
                        act.activation(dst, src, ACT.Copy).then_inc(tp_act, 1)
                elif kind == "gram":
                    r, = a
                    act.wait_ge(gp_done, GP_USES * TF + r + 1)
                    for s in range(2):
                        dst, src = gram_copy(s, r)
                        last = act.activation(dst, src, ACT.Copy)
                    last.then_inc(gp_act, 1)
                elif kind == "back":
                    k, = a
                    act.wait_ge(tp_done, TP_USES * TF + TP_BACK + k + 1)
                    act.activation(B[0:PAIR_ROWS[k], 1 + k], tp[0:PAIR_ROWS[k], (TP_BACK + k) % 2], ACT.Copy
                                   ).then_inc(tp_act, 1)
                elif kind == "x0":
                    act.activation(B[:, 0], bottom_out[:, bass.ds(TF * TILE, TILE)], ACT.Copy).then_inc(x0_hi, 1)

            act.wait_ge(small_landed, 48)
            for kind, *a in head:
                step(kind, 0, 0, *a)
            with act.Fori(0, TILES - 1) as T:
                for kind, *a in body:
                    step(kind, T, T + 1, *a)
            for kind, *a in tail:
                step(kind, TILES - 1, None, *a)

        @block.vector
        def _(dve):
            def minus_hi(dst, full, hi):
                return dve.tensor_tensor(dst, full, hi.bitcast(F32), ALU.subtract)

            def take_lo(hi, lo, emptied, par):
                dve.wait_ge(block_emptied, emptied)
                minus_hi(lo, staged[:, par], hi).then_inc(h_lo, 1)

            def step(kind, T, TF, *a):
                if kind == "raw":
                    r, = a
                    dve.wait_ge(w_hi, r + 1)
                    src, hi, lo, (p0, p1) = raw_parts(r)
                    minus_hi(lo[p0:p1], src[p0:p1], hi[p0:p1]).then_inc(w_lo, 1)
                    if r == 3:
                        dve.wait_ge(w4_hi, 1)
                        minus_hi(W4[:, 1], w4raw[:], W4[:, 0]).then_inc(w4_ready, 1)
                elif kind == "split":
                    k = a[0] % STREAM
                    TW = T if a[0] < STREAM else T + 1
                    dve.wait_ge(w_hi, raw_number(TW, k) + 1)
                    minus_hi(Wring[:, k % 2, 1], raw[:, k % 2], Wring[:, k % 2, 0]).then_inc(w_lo, 1)
                elif kind == "bottom":
                    t, b = a
                    n = bottom_number(t, b)
                    if b < BOT_SPLIT:
                        hi, lo, _ = bottom_tiles(t, b)
                        take_lo(hi, lo, n + 1, (bottom_splits(n) - 1) % 2)
                elif kind == "block":
                    b, = a
                    if b < L4:
                        hi, lo, _ = out_tiles(b)
                        take_lo(hi, lo, NB + BLOCKS * T + b + 1, b % 2)
                elif kind == "chunk":
                    c, = a
                    if TP_ENGINE[c] == "D":
                        dve.wait_ge(tp_done, TP_USES * TF + c + 1)
                        dst, src = chunk_copy(c)
                        dve.tensor_copy(dst, src).then_inc(tp_dve, 1)
                elif kind == "gram":
                    r, = a
                    dve.wait_ge(gp_done, GP_USES * TF + r + 1)
                    for s in range(2, S):
                        dst, src = gram_copy(s, r)
                        last = dve.tensor_copy(dst, src)
                    last.then_inc(gp_dve, 1)
                elif kind == "fwd":
                    f, = a
                    dve.wait_ge(tp_done, TP_USES * TF + TP_FWD + f + 1)
                    for n in range(CHUNK * f, min(CHUNK * f + CHUNK, COLS)):
                        i = n - CHUNK * f
                        src = tp[:, (TP_FWD + f) % 2, i * P:(i + 1) * P].rearrange("q (s m) -> q s m", s=S)
                        at = pair_at(n)
                        last = dve.tensor_copy(Z[:, :, at:at + COLS - n], src[:, :, n + 1:ITEMS])
                    last.then_inc(tp_dve, 1)
                elif kind == "back":
                    k, = a
                    dve.wait_ge(tp_act, TPA * TF + used("A", TP_BACK + k))
                    minus_hi(B[0:PAIR_ROWS[k], 5 + k], tp[0:PAIR_ROWS[k], (TP_BACK + k) % 2],
                             B[0:PAIR_ROWS[k], 1 + k]).then_inc(tp_dve, 1)
                elif kind == "x0":
                    dve.wait_ge(x0_hi, TF + 1)
                    minus_hi(B[:, 4], bottom_out[:, bass.ds(TF * TILE, TILE)], B[:, 0]).then_inc(x0_lo, 1)

            n_idx = TILES * UNITS * TABLES
            scratch = X[:].rearrange("p a b -> p (a b)")
            offs = scratch[:, 0:n_idx].bitcast(I32)
            wrap, clamped = scratch[:, 512:512 + n_idx], scratch[:, 1024:1024 + n_idx]
            dve.wait_ge(idx_landed, 16)
            dve.tensor_scalar(wrap, idx_all[:], 0.0, float(VOCAB), ALU.is_lt, ALU.mult).then_inc(idx_step, 1)
            dve.wait_ge(idx_step, 1)
            dve.tensor_tensor(clamped, wrap, idx_all[:], ALU.add).then_inc(idx_step, 1)
            dve.wait_ge(idx_step, 2)
            dve.tensor_scalar(clamped, clamped, 0.0, float(VOCAB - 1), ALU.max, ALU.min).then_inc(idx_step, 1)
            dve.wait_ge(idx_step, 3)
            dve.wait_ge(table_offsets, 1)
            dve.tensor_tensor(idx_all[:], clamped, offs, ALU.add).then_inc(idx_ready, 1)
            dve.wait_ge(idx_ready, 1)
            dve.memset(X[96:128], 0.0).then_inc(pads, 1)
            dve.memset(Z[:, :, PAIRS:PAIRS + 1], 0.0).then_inc(pads, 1)
            dve.wait_ge(pads, 2)
            dve.wait_ge(small_landed, 48)
            for kind, *a in head:
                step(kind, 0, 0, *a)
            with dve.Fori(0, TILES - 1) as T:
                for kind, *a in body:
                    step(kind, T, T + 1, *a)
            for kind, *a in tail:
                step(kind, TILES - 1, None, *a)

        @block.tensor
        def _(pe):
            def products(bank, k_tiles, width=TILE):
                out = mp[:, bank, 0:width]
                last_k = len(k_tiles) - 1
                for k, (whi, wlo, xhi, xlo, wait) in enumerate(k_tiles):
                    if wait:
                        pe.wait_ge(*wait)
                    o = out[0:whi.shape[1]]
                    pe.matmul(o, whi, xhi, start=(k == 0), stop=False)
                    pe.matmul(o, whi, xlo, start=False, stop=False)
                    last = pe.matmul(o, wlo, xhi, start=False, stop=(k == last_k))
                last.then_inc(block_done, 1)

            def bank_free_transpose(T, r):
                back = r - 2
                if back >= 0:
                    a, d = TPA * T + used("A", back), TPD * T + used("D", back)
                else:
                    a = TPA * T + used("A", back + TP_USES) - TPA
                    d = TPD * T + used("D", back + TP_USES) - TPD
                for s, v in ((tp_act, a), (tp_dve, d)):
                    if not isinstance(v, int) or v > 0:
                        pe.wait_ge(s, v)

            def step(kind, T, TF, *a):
                if kind == "bottom":
                    t, b = a
                    n = bottom_number(t, b)
                    if n >= 2:
                        pe.wait_ge(block_emptied, n - 1)
                    if b < 4:
                        pe.wait_ge(w_lo, 2 if t < 2 else 5)
                        pe.matmul(mp[:, n % 2, :], BW0[0:96, b * P:(b + 1) * P],
                                  XS[0:96, t * TILE:(t + 1) * TILE], start=True, stop=True).then_inc(block_done, 1)
                    elif b < 6:
                        m = b - 4
                        pe.wait_ge(w_lo, 3)
                        products(n % 2, [(Wring[:, 0, 0, k * 256 + m * P:k * 256 + (m + 1) * P],
                                          Wring[:, 0, 1, k * 256 + m * P:k * 256 + (m + 1) * P],
                                          *bottom_tiles(t, k)[:2], (h_lo, bottom_splits(bottom_number(t, k)))) for k in range(4)])
                    else:
                        pe.wait_ge(w_lo, 4)
                        products(n % 2, [(Wring[:, 1, 0, k * P:(k + 1) * P], Wring[:, 1, 1, k * P:(k + 1) * P],
                                          *bottom_tiles(t, 4 + k)[:2], (h_lo, bottom_splits(bottom_number(t, 4 + k))))
                                         for k in range(2)])
                elif kind == "block":
                    b, = a
                    n0 = NB + BLOCKS * T
                    pe.wait_ge(block_emptied, n0 + b - 1)

                    def ready(first, k):
                        return (h_lo, top_splits(T, first + k))

                    if b < L1:
                        if b == 0:
                            pe.wait_ge(x0_lo, T + 1)
                            pe.wait_ge(tp_dve, TPD * (T + 1))
                        rows = [P] + PAIR_ROWS
                        products(b % 2, [(W0[0:rows[k], 0, k, b * P:(b + 1) * P], W0[0:rows[k], 1, k, b * P:(b + 1) * P],
                                          B[0:rows[k], k], B[0:rows[k], 4 + k], None) for k in range(4)])
                    elif b < L3:
                        q = b - L1
                        pe.wait_ge(w_lo, raw_number(T, q) + 1)
                        src, first = (A, L0) if b < L2 else (B, L1)
                        start = b in (L1, L2)
                        products(b % 2, [(Wring[:, q % 2, 0, k * P:(k + 1) * P], Wring[:, q % 2, 1, k * P:(k + 1) * P],
                                          src[:, k], src[:, 8 + k], ready(first, k) if start else None)
                                         for k in range(8)])
                    elif b < L4:
                        m = b - L3
                        products(b % 2, [(W3[:, 0, k * 256 + m * P:k * 256 + (m + 1) * P],
                                          W3[:, 1, k * 256 + m * P:k * 256 + (m + 1) * P],
                                          A[:, k], A[:, 4 + k], ready(L2, k) if m == 0 else None) for k in range(4)])
                    else:
                        c = slice((b - L4) * 256, (b - L4 + 1) * 256)
                        products(b % 2, [(W4[:, 0, k:k + 1], W4[:, 1, k:k + 1], B[:, 8 + k, c], B[:, 10 + k, c],
                                          ready(L3, k) if b == L4 else None) for k in range(2)], 256)
                elif kind == "chunk":
                    c, = a
                    u, k = divmod(c, CHUNKS)
                    pe.wait_ge(gathered[k], 16 * WIDTH[k] * (UNITS * TF + u + 1))
                    bank_free_transpose(TF, c)
                    for i in range(WIDTH[k]):
                        t = CHUNK * k + i
                        last = pe.transpose(tp[:, c % 2, i * P:(i + 1) * P], G[:, t * D:(t + 1) * D], ident[:])
                    last.then_inc(tp_done, 1)
                elif kind == "gram":
                    r, = a
                    j, h = divmod(r, GRAMS)
                    if h == 0:
                        pe.wait_ge(tp_act, TPA * TF + used("A", CHUNKS * j + CHUNKS - 1))
                        pe.wait_ge(tp_dve, TPD * TF + used("D", CHUNKS * j + CHUNKS - 1))
                        pe.wait_ge(item0, UNITS * TF + j + 1)
                    if not isinstance(TF, int) or r >= 2:
                        pe.wait_ge(gp_act, GP_USES * TF + r - 1)
                        pe.wait_ge(gp_dve, GP_USES * TF + r - 1)
                    for i in range(8):
                        p = S * (8 * h + i)
                        four = E[:, j % 2, p:p + S, :]
                        last = pe.matmul(gp[0:GRAM_M, r % 2, i // 4, (i % 4) * S * COLS:(i % 4 + 1) * S * COLS],
                                         four.rearrange("d s m -> d (s m)")[:, 0:GRAM_M], four[:, :, 0:COLS],
                                         start=True, stop=True)
                    last.then_inc(gp_done, 1)
                elif kind == "fwd":
                    f, = a
                    if f == 0:
                        pe.wait_ge(gp_act, GP_USES * TF + GP_USES)
                        pe.wait_ge(gp_dve, GP_USES * TF + GP_USES)
                    bank_free_transpose(TF, TP_FWD + f)
                    for n in range(CHUNK * f, min(CHUNK * f + CHUNK, COLS)):
                        i = n - CHUNK * f
                        last = pe.transpose(tp[:, (TP_FWD + f) % 2, i * P:(i + 1) * P], X[:, n, :], ident[:])
                    last.then_inc(tp_done, 1)
                elif kind == "back":
                    k, = a
                    if k == 0:
                        pe.wait_ge(tp_dve, TPD * TF + used("D", TP_BACK - 1))
                    bank_free_transpose(TF, TP_BACK + k)
                    for s in range(S):
                        last = pe.transpose(tp[0:PAIR_ROWS[k], (TP_BACK + k) % 2, s * P:(s + 1) * P],
                                            Z[:, s, k * P:k * P + PAIR_ROWS[k]], ident[:])
                    last.then_inc(tp_done, 1)

            pe.wait_ge(consts, 2)
            pe.wait_ge(pads, 2)
            pe.wait_ge(e_pads, 1)
            for kind, *a in head:
                step(kind, 0, 0, *a)
            pe.wait_ge(w_lo, RAW_HEAD)
            pe.wait_ge(w4_ready, 1)
            with pe.Fori(0, TILES - 1) as T:
                for kind, *a in body:
                    step(kind, T, T + 1, *a)
            for kind, *a in tail:
                step(kind, TILES - 1, None, *a)


def kernel(**inputs):
    import numpy as np
    import concourse.bacc as bacc
    from concourse import mybir as mb
    from concourse.bass_utils import run_bass_kernel_spmd

    v = {k.replace("L0_rec_", ""): np.asarray(a) for k, a in inputs.items()}
    idx = v["r_categorical_inputs"].reshape(TILES, S, UNITS, P // S, TABLES).transpose(3, 1, 0, 2, 4)
    xt3 = np.zeros((96, BATCH), np.float32)
    bw03 = np.zeros((96, BOT_SIZES[0]), np.float32)
    for q in range(3):
        xt3[32 * q:32 * q + DENSE] = v["r_numerical_input"].T
        bw03[32 * q:32 * q + DENSE] = v["bw0"].T

    def k_major(w):
        out, k = w.shape
        return w.T.reshape(k // P, P, out).transpose(1, 0, 2)

    def m_blocks(w):
        out, k = w.shape
        return w.reshape(out // P, P, k // P, P).transpose(0, 3, 2, 1).reshape(out // P, P, k)

    order = [D + m * (m - 1) // 2 + n for n in range(COLS) for m in range(n + 1, ITEMS)]
    cols = list(range(D)) + order + [TOP_IN - 1]
    w0 = np.zeros((1024, 4 * P), np.float32)
    w0[:, :TOP_IN] = v["tw0"][:, cols]
    bias = np.concatenate([v[n].reshape(-1, P) for n in ("bb0", "bb1", "bb2", "tb0", "tb1", "tb2", "tb3")]).T
    arrays = {
        "idx": idx.reshape(P, -1),
        "xt": np.stack([xt3[:, :RAWC], xt3[:, RAWC:]]),
        "bw0": bw03,
        "bw1": k_major(v["bw1"]).reshape(P, -1),
        "bw2": k_major(v["bw2"]).reshape(P, -1),
        "bias": bias,
        "w4": v["tw4"].reshape(2, P).T,
        "b4": v["tb4"].reshape(1, 1),
        "wt0": k_major(w0),
        "wt3": k_major(v["tw3"]).reshape(P, -1),
        "wstream": np.concatenate([m_blocks(v["tw1"]), m_blocks(v["tw2"])]),
        "tables": v["emb_tables"].reshape(TABLES * VOCAB, D),
    }
    arrays = {k: np.ascontiguousarray(a) for k, a in arrays.items()}
    nc = bacc.Bacc("TRN2", target_bir_lowering=False, num_devices=1)
    t = {k: nc.dram_tensor(k, a.shape, mb.dt.from_np(a.dtype), kind="ExternalInput").ap() for k, a in arrays.items()}
    y = nc.dram_tensor("y", (1, BATCH), mb.dt.from_np(np.dtype("float32")), kind="ExternalOutput").ap()
    dlrm(nc, t["idx"], t["xt"], t["bw0"], t["bw1"], t["bw2"], t["bias"], t["w4"], t["b4"], t["wt0"], t["wt3"],
         t["wstream"], t["tables"], y)
    r = run_bass_kernel_spmd(nc, [arrays], core_ids=[0])
    return r.results[0]["y"].reshape(BATCH, 1)
```

```python
from contextlib import ExitStack

import concourse.bass as bass
from concourse import mybir

ALU = mybir.AluOpType
ACT = mybir.ActivationFunctionType
F32 = mybir.dt.float32
F32R = mybir.dt.float32r
I32 = mybir.dt.int32

P = 128
BATCH = 2048
TILE = 512
TILES = BATCH // TILE
SEG_UNITS = [2, 2, 4, 4, 4]
SEGS = len(SEG_UNITS)
LOOP = (2, 4)
UNITS = BATCH // P
FIRST_UNIT = [sum(SEG_UNITS[:s]) for s in range(SEGS)]
WIDE = [P * n for n in SEG_UNITS]
BASE = [P * n for n in FIRST_UNIT]
TABLES = 26
VOCAB = 12500
D = 128
ITEMS = TABLES + 1
ITEM_PITCH = 32
PAIRS = ITEMS * (ITEMS - 1) // 2
TOP_IN = D + PAIRS + 1
DENSE = 13
S = 4
GRAM_M = (S - 1) * ITEM_PITCH + ITEMS
COLS = ITEMS - 1

CHUNK = 4
CHUNKS = -(-TABLES // CHUNK)
WIDTH = [min(CHUNK, TABLES - CHUNK * k) for k in range(CHUNKS)]
GRAMS = 4
FWDS = -(-COLS // CHUNK)
PAIR_TILES = 3
PAIR_ROWS = [P, P, PAIRS + 1 - 2 * P]

BOT_SIZES = [512, 256, 128]
BOT_BLOCKS = 7
NB = TILES * BOT_BLOCKS
BOT_SPLIT = 6
L0, L1, L2, L3, L4 = 0, 8, 16, 20, 22
BLOCKS = 24
STREAM = 12
RAW_HEAD = 10
RAWC = 1024


def pair_at(n):
    return sum(ITEMS - 1 - i for i in range(n))


def unit_segment(U):
    return max(s for s in range(SEGS) if FIRST_UNIT[s] <= U)


def top_blocks(seg):
    return BLOCKS if WIDE[seg] == TILE else BLOCKS - 1



def front_steps(seg):
    steps, late = [], []
    for U in range(FIRST_UNIT[seg], FIRST_UNIT[seg] + SEG_UNITS[seg]):
        for k in range(CHUNKS):
            steps.append(("chunk", U, k))
            if late and k in (1, 2, 4, 5):
                steps.append(late.pop(0))
        late = [("gram", U, h) for h in range(GRAMS)]
    return steps + late


def fwd_steps(seg, a, b):
    return [("fwd", seg, f) for f in range(a, b)]


def back_steps(seg):
    return [("back", seg, k) for k in range(PAIR_TILES)] + [("x0", seg)]


def weave(blocks, front, lead):
    cost = [1 if b[2] < L1 else 2 for b in blocks]
    whole, done, put = len(front), 0, lead
    steps = front[:lead]
    for b, c in zip(blocks, cost):
        steps.append(b)
        done += c
        upto = lead + round((whole - lead) * done / sum(cost))
        steps += front[put:upto]
        put = upto
    return steps


def head_schedule():
    def first(t, b):
        return [("bottom", t, b)] if t < TILES else []

    bottoms = [("bottom", 0, b) for b in range(4)]
    for t in range(TILES):
        bottoms += [("bottom", t, 4)] + first(t + 1, 0) + first(t + 1, 1)
        bottoms += [("bottom", t, 5)] + first(t + 1, 2) + first(t + 1, 3) + [("bottom", t, 6)]
    at = {("bottom", 0, 3): [("raw", 3), ("pads",)], ("bottom", 0, 4): [("raw", 4)], ("bottom", 0, 6): [("raw", 5)],
          ("bottom", 1, 6): [("raw", 6)], ("bottom", 2, 4): [("raw", 7)], ("bottom", 2, 6): [("raw", 8)],
          ("bottom", 3, 4): [("raw", 9)]}
    front = front_steps(0)
    steps = [("raw", r) for r in range(3)]
    for i, b in enumerate(bottoms):
        steps.append(b)
        steps += at.get(b, [])
        if i >= 10 and i % 2 == 0:
            steps.append(front.pop(0))
    steps += [("split", 0, 0), ("split", 0, 1)] + front
    return steps + fwd_steps(0, 0, FWDS) + back_steps(0)


def segment_schedule(seg):
    blocks = [("block", seg, b) for b in range(top_blocks(seg))]
    nxt = seg + 1 if seg + 1 < SEGS else None
    front = front_steps(nxt) if nxt else []
    steps = weave(blocks[:L3 - 2], front, 3 if nxt else 0)
    if nxt:
        steps += [blocks[18]] + fwd_steps(nxt, 0, 2) + [blocks[19]] + fwd_steps(nxt, 2, 4)
        steps += [blocks[20]] + fwd_steps(nxt, 4, 6) + [blocks[21]] + fwd_steps(nxt, 6, FWDS)
        steps += [blocks[22]] + back_steps(nxt) + blocks[23:]
    else:
        steps += blocks[18:]
    out = []
    for st in steps:
        out.append(st)
        if st[0] == "block" and L1 <= st[2] < L3:
            k = st[2] - L1 + 2
            if k < STREAM:
                out.append(("split", seg, k))
            elif nxt:
                out.append(("split", nxt, k - STREAM))
    return out


SCHEDULE = [head_schedule()] + [segment_schedule(s) for s in range(SEGS)]


def emptied_by(step):
    if step[0] == "chunk":
        return "D" if (CHUNKS * (step[1] % 4) + step[2]) % 3 == 2 else "A"
    if step[0] == "fwd":
        return "A" if step[2] % 3 == 1 else "D"
    return "B"


def number_steps():
    tp_at, tp_a, tp_d, blk_at, split_at = {}, {}, {}, {}, {}
    a = d = 0
    for st in (st for part in SCHEDULE for st in part):
        if st[0] in ("chunk", "fwd", "back"):
            tp_at[st] = len(tp_at) + 1
            a += emptied_by(st) in "AB"
            d += emptied_by(st) in "DB"
            tp_a[tp_at[st]], tp_d[tp_at[st]] = a, d
        elif st[0] in ("bottom", "block"):
            blk_at[st] = len(blk_at) + 1
            if st[2] < (BOT_SPLIT if st[0] == "bottom" else L4):
                split_at[st] = len(split_at) + 1
    return tp_at, tp_a, tp_d, blk_at, split_at


TP_AT, TP_A, TP_D, BLK_AT, SPLIT_AT = number_steps()

_a, _b = ("fwd", LOOP[0] + 1, 0), ("fwd", LOOP[0] + 2, 0)
PER_TP = TP_AT[_b] - TP_AT[_a]
PER_A = TP_A[TP_AT[_b]] - TP_A[TP_AT[_a]]
PER_D = TP_D[TP_AT[_b]] - TP_D[TP_AT[_a]]
PER_UNITS = SEG_UNITS[LOOP[0]]
PER_BLK = BLOCKS
PER_SPLIT = L4
PER_GP = GRAMS * PER_UNITS
assert not any(n % 2 for n in (PER_TP, PER_UNITS, PER_BLK, PER_SPLIT, PER_GP, STREAM))


def raw_number(seg, k):
    return RAW_HEAD + STREAM * seg + k + 1


def dlrm(nc, idx, xt, bw0, bw1, bw2, bias, w4, b4, wt0, wt3, wstream, tables, y):
    with ExitStack() as ctx:
        def sb(name, shape, dt):
            return ctx.enter_context(nc.sbuf_tensor(name, shape, dt))

        def sem(name):
            return ctx.enter_context(nc.semaphore(name))

        W0 = sb("W0", [P, 2, 4, 1024], F32R)
        W3 = sb("W3", [P, 2, RAWC], F32R)
        W4 = sb("W4", [P, 2, 2], F32R)
        Wring = sb("Wring", [P, 2, 2, RAWC], F32R)
        raw = sb("raw", [P, 2, RAWC], F32)
        w4raw = sb("w4raw", [P, 2], F32)
        A = sb("A", [P, 16, TILE], F32R)
        B = sb("B", [P, 16, TILE], F32R)
        staged = sb("staged", [P, 2, TILE], F32)
        bottom_out = sb("bottom_out", [P, BATCH], F32)
        biases = sb("biases", [P, 29], F32)
        bias4 = sb("bias4", [1, 1], F32)
        G = sb("G", [P, TABLES * D], F32)
        E = sb("E", [P, 2, P, ITEM_PITCH], F32)
        X = sb("X", [P, COLS, P], F32)
        Z = sb("Z", [P, S, PAIRS + 1], F32)
        ident = sb("ident", [P, P], F32)
        idx_all = sb("idx_all", [P, UNITS * TABLES], I32)
        idx_unit = sb("idx_unit", [P, 2, TABLES], I32)

        tp = ctx.enter_context(nc.psum_tensor("tp", [P, 2, 512], F32))
        gp = ctx.enter_context(nc.psum_tensor("gp", [P, 2, 2, 512], F32))
        mp = ctx.enter_context(nc.psum_tensor("mp", [P, 2, 512], F32))

        XS = B[:, 8:12, :].rearrange("p a b -> p (a b)")
        BW0 = B[:, 12, :]

        idx_landed = sem("idx_landed")
        small_landed = sem("small_landed")
        raw_landed = [sem(f"raw_landed{i}") for i in range(2)]
        table_offsets = sem("table_offsets")
        consts = sem("consts")
        pads = sem("pads")
        idx_step = sem("idx_step")
        idx_ready = sem("idx_ready")
        idx_copied = sem("idx_copied")
        gather_turn = sem("gather_turn")
        gathered = [sem(f"gathered{k}") for k in range(CHUNKS)]
        w_hi, w_lo, w4_ready = sem("w_hi"), sem("w_lo"), sem("w4_ready")
        w4_hi = sem("w4_hi")
        tp_done, tp_act, tp_dve = sem("tp_done"), sem("tp_act"), sem("tp_dve")
        item0 = sem("item0")
        gp_done, gp_act, gp_dve = sem("gp_done"), sem("gp_act"), sem("gp_dve")
        x0_hi, x0_lo = sem("x0_hi"), sem("x0_lo")
        block_done = sem("block_done")
        block_emptied, h_lo = sem("block_emptied"), sem("h_lo")
        y_stored = sem("y_stored")

        block = ctx.enter_context(nc.Block())

        def run(engine, step):
            for part in SCHEDULE[:LOOP[0] + 1]:
                for kind, *a in part:
                    step(None, kind, *a)
            with engine.Fori(0, LOOP[1] - LOOP[0]) as it:
                for kind, *a in SCHEDULE[LOOP[0] + 1]:
                    step(it, kind, *a)
            for part in SCHEDULE[LOOP[1] + 1:]:
                for kind, *a in part:
                    step(None, kind, *a)

        def at(it, n, per):
            return n if it is None else n + it * per

        @block.sync
        def _(sp):
            sp.dma_start(idx_all[:], idx).then_inc(idx_landed, 16)
            loads = [(raw[0:96, 0, 0:512], bw0), (raw[0:96, 1, :], xt[0]),
                     (raw[:, 0, :], bw1), (raw[:, 1, 0:256], bw2), (raw[0:96, 0, :], xt[1])]
            loads += [(raw[:, (5 + k) % 2, :], wt0[:, k, :]) for k in range(4)]
            loads += [(raw[:, 1, :], wt3)]
            for r, (dst, src) in enumerate(loads):
                if r >= 2:
                    sp.wait_ge(w_lo, r - 1)
                sp.dma_start(dst, src).then_inc(raw_landed[r % 2], 16)
                if r == 1:
                    sp.dma_start(biases[:], bias).then_inc(small_landed, 16)
                    sp.dma_start(w4raw[:], w4).then_inc(small_landed, 16)
                    sp.dma_start(bias4[:], b4).then_inc(small_landed, 16)
            for k in range(2):
                sp.wait_ge(w_lo, raw_number(0, k) - 2)
                sp.dma_start(raw[:, k, :], wstream[k]).then_inc(raw_landed[k], 16)

            def reload(seg, k):
                sp.wait_ge(w_lo, seg * STREAM + raw_number(0, k))
                sp.dma_start(raw[:, k % 2, :], wstream[(k + 2) % STREAM]).then_inc(raw_landed[k % 2], 16)

            with sp.Fori(0, SEGS - 1) as seg:
                for k in range(STREAM):
                    reload(seg, k)
            for k in range(STREAM - 2):
                reload(SEGS - 1, k)
            sp.wait_ge(block_emptied, len(BLK_AT))
            sp.dma_start(y, bottom_out[0:1, :]).then_inc(y_stored, 16)
            sp.wait_ge(y_stored, 16)

        @block.gpsimd
        def _(pool):
            offs = X[:, 0:4, :].rearrange("p a b -> p (a b)").bitcast(I32)[:, 0:UNITS * TABLES]
            pool.iota(offs.rearrange("p (a t) -> p a t", t=TABLES), pattern=[[0, UNITS], [VOCAB, TABLES]],
                      base=0, channel_multiplier=0).then_inc(table_offsets, 1)
            pool.memset(ident[:], 0.0).then_inc(consts, 1)
            pool.wait_ge(consts, 1)
            pool.affine_select(out=ident[:], in_=ident[:], compare_op=ALU.not_equal, fill=1.0, base=0,
                               pattern=[[-1, P]], channel_multiplier=1).then_inc(consts, 1)
            pool.wait_ge(idx_ready, 1)

            def copy_indices(U, par):
                pool.tensor_copy(idx_unit[:, par, :], idx_all[:, bass.ds(U * TABLES, TABLES)]).then_inc(idx_copied, 1)
                pool.wait_ge(idx_copied, U + 1)
                pool.sem_inc(gather_turn, 1)

            def gather_unit(U, it=None):
                for k in range(CHUNKS):
                    if U > 0:
                        pool.wait_ge(tp_done, at(it, TP_AT["chunk", U - 1, k], PER_TP))
                    if k == 0:
                        copy_indices(at(it, U, PER_UNITS), U % 2)
                    else:
                        pool.sem_inc(gather_turn, 1)
                    for i in range(WIDTH[k]):
                        t = CHUNK * k + i
                        pool.indirect_dma_start(G[:, t * D:(t + 1) * D], None, tables,
                                                bass.IndirectOffsetOnAxis(idx_unit[:, U % 2, t:t + 1], 0)
                                                ).then_inc(gathered[k], 16)

            first = FIRST_UNIT[LOOP[0] + 1] + 1
            for U in range(first):
                gather_unit(U)
            with pool.Fori(0, LOOP[1] - LOOP[0] - 1) as it:
                for U in range(first, first + PER_UNITS):
                    gather_unit(U, it)
            for U in range(first + PER_UNITS * (LOOP[1] - LOOP[0] - 1), UNITS):
                gather_unit(U)

        def segment_out(seg, it):
            return bottom_out[:, bass.ds(at(it, BASE[seg], TILE), WIDE[seg])]

        def item0_source(U, it):
            seg = unit_segment(U)
            src = segment_out(seg, it).rearrange("d (s j g) -> d j g s", s=S, j=SEG_UNITS[seg])
            return src[:, U - FIRST_UNIT[seg]]

        def gram_copy(s, U, h):
            rows = ITEM_PITCH if s < S - 1 else ITEMS
            q = 32 * (U - FIRST_UNIT[unit_segment(U)]) + 8 * h
            src = gp[32 * s:32 * s + rows, h % 2, :, 0:4 * S * COLS]
            src = src.rearrange("p b (i c) -> p b i c", c=S * COLS)[:, :, :, s * COLS:(s + 1) * COLS]
            dst = X[32 * s:32 * s + rows, :, q:q + 8]
            return dst.rearrange("p n (b i) -> p b i n", b=2), src

        def tp_bank(st):
            return (TP_AT[st] - 1) % 2

        def chunk_copy(U, k):
            dst = E[:, U % 2, :, 1 + CHUNK * k:1 + CHUNK * k + WIDTH[k]].rearrange("d p i -> d i p")
            src = tp[:, tp_bank(("chunk", U, k)), 0:WIDTH[k] * P]
            return dst, src.rearrange("d (i p) -> d i p", i=WIDTH[k])

        def fwd_copies(seg, f):
            rows = WIDE[seg] // S
            for n in range(CHUNK * f, min(CHUNK * f + CHUNK, COLS)):
                i = n - CHUNK * f
                src = tp[0:rows, tp_bank(("fwd", seg, f)), i * P:(i + 1) * P].rearrange("q (s m) -> q s m", s=S)
                yield Z[0:rows, :, pair_at(n):pair_at(n) + COLS - n], src[:, :, n + 1:ITEMS]

        def out_tiles(b):
            if b < L1:
                return A[:, b], A[:, 8 + b], 7 + b
            if b < L2:
                return B[:, b - L1], B[:, 8 + b - L1], 7 + b
            if b < L3:
                return A[:, b - L2], A[:, 4 + b - L2], 7 + b
            return B[:, 8 + b - L3], B[:, 10 + b - L3], 7 + b

        def bottom_tiles(t, b):
            if b < 4:
                return A[:, 8 * (t % 2) + b], A[:, 8 * (t % 2) + 4 + b], b
            return B[:, 4 * (t % 2) + b - 4], B[:, 4 * (t % 2) + b - 2], b

        def raw_parts(r):
            if r == 0:
                return raw[0:96, 0, 0:512], BW0[0:96], BW0, (32, 64)
            if r in (1, 4):
                half = XS[:, RAWC * (r // 4):RAWC * (r // 4 + 1)]
                return raw[0:96, r % 2, :], half[0:96], half, (64, 96)
            if r == 2:
                return raw[:, 0, :], Wring[:, 0, 0, :], Wring[:, 0, 1, :], (0, P)
            if r == 3:
                return raw[:, 1, 0:256], Wring[:, 1, 0, 0:256], Wring[:, 1, 1, 0:256], (0, P)
            if r < 9:
                return raw[:, r % 2, :], W0[:, 0, r - 5], W0[:, 1, r - 5], (0, P)
            return raw[:, 1, :], W3[:, 0], W3[:, 1], (0, P)

        def slot_used(seg, k):
            if seg == 0 and k < 2:
                return NB
            return BLK_AT["block", seg, L1 + k - 2] if k >= 2 else BLK_AT["block", seg - 1, L3 + k - 2]

        @block.scalar
        def _(act):
            def empty_split(it, st, hi, col, w):
                n, ns = BLK_AT[st], SPLIT_AT[st]
                act.wait_ge(block_done, at(it, n, PER_BLK))
                src, b = mp[:, (n - 1) % 2, 0:w], biases[:, col:col + 1]
                act.activation(hi[:, 0:w], src, ACT.Relu, bias=b)
                if ns > 2:
                    act.wait_ge(h_lo, at(it, ns - 2, PER_SPLIT))
                act.activation(staged[:, (ns - 1) % 2, 0:w], src, ACT.Relu, bias=b).then_inc(block_emptied, 1)

            def step(it, kind, *a):
                st = (kind, *a)
                if kind == "raw":
                    r, = a
                    act.wait_ge(raw_landed[r % 2], 16 * (r // 2 + 1))
                    src, hi, _, _ = raw_parts(r)
                    act.activation(hi, src, ACT.Copy).then_inc(w_hi, 1)
                    if r == 3:
                        act.activation(W4[:, 0], w4raw[:], ACT.Copy).then_inc(w4_hi, 1)
                elif kind == "split":
                    seg, k = a
                    act.wait_ge(raw_landed[k % 2], at(it, 16 * ((raw_number(seg, k) - 1) // 2 + 1), 16 * STREAM // 2))
                    act.wait_ge(block_done, at(it, slot_used(seg, k), PER_BLK))
                    act.activation(Wring[:, k % 2, 0], raw[:, k % 2], ACT.Copy).then_inc(w_hi, 1)
                elif kind == "bottom":
                    t, b = a
                    if b < BOT_SPLIT:
                        hi, _, col = bottom_tiles(t, b)
                        empty_split(None, st, hi, col, TILE)
                    else:
                        act.wait_ge(block_done, BLK_AT[st])
                        act.activation(bottom_out[:, t * TILE:(t + 1) * TILE], mp[:, (BLK_AT[st] - 1) % 2, :], ACT.Relu,
                                       bias=biases[:, 6:7]).then_inc(block_emptied, 1)
                elif kind == "block":
                    seg, b = a
                    if b < L4:
                        hi, _, col = out_tiles(b)
                        empty_split(it, st, hi, col, WIDE[seg])
                    else:
                        act.wait_ge(block_done, at(it, BLK_AT[st], PER_BLK))
                        act.activation(bottom_out[0:1, bass.ds(at(it, BASE[seg] + (b - L4) * 256, TILE), 256)],
                                       mp[0:1, (BLK_AT[st] - 1) % 2, 0:256], ACT.Identity, bias=bias4[:]
                                       ).then_inc(block_emptied, 1)
                elif kind == "chunk":
                    U, k = a
                    if k == 0:
                        act.wait_ge(tp_done, at(it, TP_AT[st], PER_TP))
                        tile = BASE[unit_segment(U)] // TILE
                        act.wait_ge(block_emptied, BLK_AT["bottom", tile if it is None else TILES - 1, 6])
                        act.activation(E[:, U % 2, :, 0].rearrange("d (g s) -> d g s", s=S),
                                       item0_source(U, it), ACT.Copy).then_inc(item0, 1)
                    if emptied_by(st) == "A":
                        act.wait_ge(tp_done, at(it, TP_AT[st], PER_TP))
                        dst, src = chunk_copy(U, k)
                        act.activation(dst, src, ACT.Copy).then_inc(tp_act, 1)
                elif kind == "gram":
                    U, h = a
                    act.wait_ge(gp_done, at(it, GRAMS * U + h + 1, PER_GP))
                    for s in range(2):
                        dst, src = gram_copy(s, U, h)
                        last = act.activation(dst, src, ACT.Copy)
                    last.then_inc(gp_act, 1)
                elif kind == "fwd" and emptied_by(st) == "A":
                    act.wait_ge(tp_done, at(it, TP_AT[st], PER_TP))
                    for dst, src in fwd_copies(*a):
                        last = act.activation(dst, src, ACT.Copy)
                    last.then_inc(tp_act, 1)
                elif kind == "back":
                    seg, k = a
                    act.wait_ge(tp_done, at(it, TP_AT[st], PER_TP))
                    act.activation(B[0:PAIR_ROWS[k], 1 + k, 0:WIDE[seg]], tp[0:PAIR_ROWS[k], tp_bank(st), 0:WIDE[seg]],
                                   ACT.Copy).then_inc(tp_act, 1)
                elif kind == "x0":
                    seg, = a
                    act.activation(B[:, 0, 0:WIDE[seg]], segment_out(seg, it), ACT.Copy).then_inc(x0_hi, 1)

            act.wait_ge(small_landed, 48)
            run(act, step)

        @block.vector
        def _(dve):
            def minus_hi(dst, full, hi):
                return dve.tensor_tensor(dst, full, hi.bitcast(F32), ALU.subtract)

            def take_lo(it, st, hi, lo, w):
                dve.wait_ge(block_emptied, at(it, BLK_AT[st], PER_BLK))
                minus_hi(lo[:, 0:w], staged[:, (SPLIT_AT[st] - 1) % 2, 0:w], hi[:, 0:w]).then_inc(h_lo, 1)

            def step(it, kind, *a):
                st = (kind, *a)
                if kind == "raw":
                    r, = a
                    dve.wait_ge(w_hi, r + 1)
                    src, hi, lo, (p0, p1) = raw_parts(r)
                    minus_hi(lo[p0:p1], src[p0:p1], hi[p0:p1]).then_inc(w_lo, 1)
                    if r == 3:
                        dve.wait_ge(w4_hi, 1)
                        minus_hi(W4[:, 1], w4raw[:], W4[:, 0]).then_inc(w4_ready, 1)
                elif kind == "pads":
                    dve.wait_ge(idx_ready, 1)
                    dve.memset(X[96:128], 0.0).then_inc(pads, 1)
                    dve.memset(E[:, :, :, ITEMS:ITEM_PITCH], 0.0).then_inc(pads, 1)
                    dve.memset(Z[:, :, PAIRS:PAIRS + 1], 0.0).then_inc(pads, 1)
                elif kind == "split":
                    seg, k = a
                    dve.wait_ge(w_hi, at(it, raw_number(seg, k), STREAM))
                    minus_hi(Wring[:, k % 2, 1], raw[:, k % 2], Wring[:, k % 2, 0]).then_inc(w_lo, 1)
                elif kind == "bottom":
                    t, b = a
                    if b < BOT_SPLIT:
                        hi, lo, _ = bottom_tiles(t, b)
                        take_lo(None, st, hi, lo, TILE)
                elif kind == "block":
                    seg, b = a
                    if b < L4:
                        hi, lo, _ = out_tiles(b)
                        take_lo(it, st, hi, lo, WIDE[seg])
                elif kind == "chunk":
                    if emptied_by(st) == "D":
                        dve.wait_ge(tp_done, at(it, TP_AT[st], PER_TP))
                        dst, src = chunk_copy(*a)
                        dve.tensor_copy(dst, src).then_inc(tp_dve, 1)
                elif kind == "gram":
                    U, h = a
                    if U == 0 and h == 0:
                        dve.wait_ge(pads, 1)
                    dve.wait_ge(gp_done, at(it, GRAMS * U + h + 1, PER_GP))
                    for s in range(2, S):
                        dst, src = gram_copy(s, U, h)
                        last = dve.tensor_copy(dst, src)
                    last.then_inc(gp_dve, 1)
                elif kind == "fwd" and emptied_by(st) == "D":
                    dve.wait_ge(tp_done, at(it, TP_AT[st], PER_TP))
                    for dst, src in fwd_copies(*a):
                        last = dve.tensor_copy(dst, src)
                    last.then_inc(tp_dve, 1)
                elif kind == "back":
                    seg, k = a
                    dve.wait_ge(tp_act, at(it, TP_A[TP_AT[st]], PER_A))
                    minus_hi(B[0:PAIR_ROWS[k], 5 + k, 0:WIDE[seg]], tp[0:PAIR_ROWS[k], tp_bank(st), 0:WIDE[seg]],
                             B[0:PAIR_ROWS[k], 1 + k, 0:WIDE[seg]]).then_inc(tp_dve, 1)
                elif kind == "x0":
                    seg, = a
                    dve.wait_ge(x0_hi, at(it, seg + 1, 1))
                    minus_hi(B[:, 4, 0:WIDE[seg]], segment_out(seg, it), B[:, 0, 0:WIDE[seg]]).then_inc(x0_lo, 1)

            n_idx = UNITS * TABLES
            scratch = X[:].rearrange("p a b -> p (a b)")
            offs = scratch[:, 0:n_idx].bitcast(I32)
            wrap, clamped = scratch[:, 512:512 + n_idx], scratch[:, 1024:1024 + n_idx]
            dve.wait_ge(idx_landed, 16)
            dve.tensor_scalar(wrap, idx_all[:], 0.0, float(VOCAB), ALU.is_lt, ALU.mult).then_inc(idx_step, 1)
            dve.wait_ge(idx_step, 1)
            dve.tensor_tensor(clamped, wrap, idx_all[:], ALU.add).then_inc(idx_step, 1)
            dve.wait_ge(idx_step, 2)
            dve.tensor_scalar(clamped, clamped, 0.0, float(VOCAB - 1), ALU.max, ALU.min).then_inc(idx_step, 1)
            dve.wait_ge(idx_step, 3)
            dve.wait_ge(table_offsets, 1)
            dve.tensor_tensor(idx_all[:], clamped, offs, ALU.add).then_inc(idx_ready, 1)
            dve.wait_ge(small_landed, 48)
            run(dve, step)

        @block.tensor
        def _(pe):
            def products(st, k_tiles, width=TILE):
                out = mp[:, (BLK_AT[st] - 1) % 2, 0:width]
                last_k = len(k_tiles) - 1
                for k, (whi, wlo, xhi, xlo, wait) in enumerate(k_tiles):
                    if wait:
                        pe.wait_ge(*wait)
                    o = out[0:whi.shape[1]]
                    pe.matmul(o, whi, xhi, start=(k == 0), stop=False)
                    pe.matmul(o, whi, xlo, start=False, stop=False)
                    last = pe.matmul(o, wlo, xhi, start=False, stop=(k == last_k))
                last.then_inc(block_done, 1)

            def wait_for_bank(it, st):
                last = TP_AT[st] - 2
                if last < 1:
                    return
                who = next(emptied_by(x) for x, n in TP_AT.items() if n == last)
                if who == "A":
                    pe.wait_ge(tp_act, at(it, TP_A[last], PER_A))
                else:
                    pe.wait_ge(tp_dve, at(it, TP_D[last], PER_D))

            def step(it, kind, *a):
                st = (kind, *a)
                if kind in ("bottom", "block") and BLK_AT[st] > 2:
                    pe.wait_ge(block_emptied, at(it, BLK_AT[st] - 2, PER_BLK))
                if kind == "bottom":
                    t, b = a
                    if b < 4:
                        pe.wait_ge(w_lo, 2 if t < 2 else 5)
                        pe.matmul(mp[:, (BLK_AT[st] - 1) % 2, :], BW0[0:96, b * P:(b + 1) * P],
                                  XS[0:96, t * TILE:(t + 1) * TILE], start=True, stop=True).then_inc(block_done, 1)
                    elif b < 6:
                        m = b - 4
                        pe.wait_ge(w_lo, 3)
                        products(st, [(Wring[:, 0, 0, k * 256 + m * P:k * 256 + (m + 1) * P],
                                       Wring[:, 0, 1, k * 256 + m * P:k * 256 + (m + 1) * P],
                                       *bottom_tiles(t, k)[:2], (h_lo, SPLIT_AT["bottom", t, k])) for k in range(4)])
                    else:
                        pe.wait_ge(w_lo, 4)
                        products(st, [(Wring[:, 1, 0, k * P:(k + 1) * P], Wring[:, 1, 1, k * P:(k + 1) * P],
                                       *bottom_tiles(t, 4 + k)[:2], (h_lo, SPLIT_AT["bottom", t, 4 + k]))
                                      for k in range(2)])
                elif kind == "block":
                    seg, b = a
                    w = WIDE[seg]

                    def ready(first, k):
                        return (h_lo, at(it, SPLIT_AT["block", seg, first + k], PER_SPLIT))

                    if b < L1:
                        if b == 0:
                            pe.wait_ge(w_lo, RAW_HEAD)
                            pe.wait_ge(x0_lo, at(it, seg + 1, 1))
                            pe.wait_ge(tp_dve, at(it, TP_D[TP_AT["back", seg, PAIR_TILES - 1]], PER_D))
                        rows = [P] + PAIR_ROWS
                        products(st, [(W0[0:rows[k], 0, k, b * P:(b + 1) * P], W0[0:rows[k], 1, k, b * P:(b + 1) * P],
                                       B[0:rows[k], k, 0:w], B[0:rows[k], 4 + k, 0:w], None) for k in range(4)], w)
                    elif b < L3:
                        q = b - L1
                        pe.wait_ge(w_lo, at(it, raw_number(seg, q), STREAM))
                        src, first = (A, L0) if b < L2 else (B, L1)
                        start = b in (L1, L2)
                        products(st, [(Wring[:, q % 2, 0, k * P:(k + 1) * P], Wring[:, q % 2, 1, k * P:(k + 1) * P],
                                       src[:, k, 0:w], src[:, 8 + k, 0:w], ready(first, k) if start else None)
                                      for k in range(8)], w)
                    elif b < L4:
                        m = b - L3
                        products(st, [(W3[:, 0, k * 256 + m * P:k * 256 + (m + 1) * P],
                                       W3[:, 1, k * 256 + m * P:k * 256 + (m + 1) * P],
                                       A[:, k, 0:w], A[:, 4 + k, 0:w], ready(L2, k) if m == 0 else None)
                                      for k in range(4)], w)
                    else:
                        if seg == 0:
                            pe.wait_ge(w4_ready, 1)
                        c = slice((b - L4) * 256, (b - L4 + 1) * 256)
                        products(st, [(W4[:, 0, k:k + 1], W4[:, 1, k:k + 1], B[:, 8 + k, c], B[:, 10 + k, c],
                                       ready(L3, k) if b == L4 else None) for k in range(2)], 256)
                elif kind == "chunk":
                    U, k = a
                    pe.wait_ge(gathered[k], at(it, 16 * WIDTH[k] * (U + 1), 16 * WIDTH[k] * PER_UNITS))
                    wait_for_bank(it, st)
                    for i in range(WIDTH[k]):
                        t = CHUNK * k + i
                        last = pe.transpose(tp[:, tp_bank(st), i * P:(i + 1) * P], G[:, t * D:(t + 1) * D], ident[:])
                    last.then_inc(tp_done, 1)
                elif kind == "gram":
                    U, h = a
                    if U == 0 and h == 0:
                        pe.wait_ge(pads, 3)
                    if h == 0:
                        n = TP_AT["chunk", U, CHUNKS - 1]
                        pe.wait_ge(tp_act, at(it, TP_A[n], PER_A))
                        pe.wait_ge(tp_dve, at(it, TP_D[n], PER_D))
                        pe.wait_ge(item0, at(it, U + 1, PER_UNITS))
                    if GRAMS * U + h >= 2:
                        pe.wait_ge(gp_act, at(it, GRAMS * U + h - 1, PER_GP))
                        pe.wait_ge(gp_dve, at(it, GRAMS * U + h - 1, PER_GP))
                    for i in range(8):
                        p = S * (8 * h + i)
                        four = E[:, U % 2, p:p + S, :]
                        last = pe.matmul(gp[0:GRAM_M, h % 2, i // 4, (i % 4) * S * COLS:(i % 4 + 1) * S * COLS],
                                         four.rearrange("d s m -> d (s m)")[:, 0:GRAM_M], four[:, :, 0:COLS],
                                         start=True, stop=True)
                    last.then_inc(gp_done, 1)
                elif kind == "fwd":
                    seg, f = a
                    if f == 0:
                        n = GRAMS * (FIRST_UNIT[seg] + SEG_UNITS[seg])
                        pe.wait_ge(gp_act, at(it, n, PER_GP))
                        pe.wait_ge(gp_dve, at(it, n, PER_GP))
                    wait_for_bank(it, st)
                    rows = WIDE[seg] // S
                    for n in range(CHUNK * f, min(CHUNK * f + CHUNK, COLS)):
                        i = n - CHUNK * f
                        last = pe.transpose(tp[0:rows, tp_bank(st), i * P:(i + 1) * P], X[:, n, 0:rows], ident[:])
                    last.then_inc(tp_done, 1)
                elif kind == "back":
                    seg, k = a
                    if k == 0:
                        n = TP_AT["fwd", seg, FWDS - 1]
                        pe.wait_ge(tp_act, at(it, TP_A[n], PER_A))
                        pe.wait_ge(tp_dve, at(it, TP_D[n], PER_D))
                    wait_for_bank(it, st)
                    rows = WIDE[seg] // S
                    for s in range(S):
                        last = pe.transpose(tp[0:PAIR_ROWS[k], tp_bank(st), s * rows:(s + 1) * rows],
                                            Z[0:rows, s, k * P:k * P + PAIR_ROWS[k]], ident[0:rows, 0:rows])
                    last.then_inc(tp_done, 1)

            pe.wait_ge(consts, 2)
            run(pe, step)


def kernel(**inputs):
    import numpy as np
    import concourse.bacc as bacc
    from concourse import mybir as mb
    from concourse.bass_utils import run_bass_kernel_spmd

    v = {k.replace("L0_rec_", ""): np.asarray(a) for k, a in inputs.items()}
    idx = [v["r_categorical_inputs"][b:b + w].reshape(S, n, P // S, TABLES).transpose(2, 0, 1, 3).reshape(P, -1)
           for b, w, n in zip(BASE, WIDE, SEG_UNITS)]
    xt3 = np.zeros((96, BATCH), np.float32)
    bw03 = np.zeros((96, BOT_SIZES[0]), np.float32)
    for q in range(3):
        xt3[32 * q:32 * q + DENSE] = v["r_numerical_input"].T
        bw03[32 * q:32 * q + DENSE] = v["bw0"].T

    def k_major(w):
        out, k = w.shape
        return w.T.reshape(k // P, P, out).transpose(1, 0, 2)

    def m_blocks(w):
        out, k = w.shape
        return w.reshape(out // P, P, k // P, P).transpose(0, 3, 2, 1).reshape(out // P, P, k)

    order = [D + m * (m - 1) // 2 + n for n in range(COLS) for m in range(n + 1, ITEMS)]
    cols = list(range(D)) + order + [TOP_IN - 1]
    w0 = np.zeros((1024, 4 * P), np.float32)
    w0[:, :TOP_IN] = v["tw0"][:, cols]
    bias = np.concatenate([v[n].reshape(-1, P) for n in ("bb0", "bb1", "bb2", "tb0", "tb1", "tb2", "tb3")]).T
    arrays = {
        "idx": np.concatenate(idx, axis=1),
        "xt": np.stack([xt3[:, :RAWC], xt3[:, RAWC:]]),
        "bw0": bw03,
        "bw1": k_major(v["bw1"]).reshape(P, -1),
        "bw2": k_major(v["bw2"]).reshape(P, -1),
        "bias": bias,
        "w4": v["tw4"].reshape(2, P).T,
        "b4": v["tb4"].reshape(1, 1),
        "wt0": k_major(w0),
        "wt3": k_major(v["tw3"]).reshape(P, -1),
        "wstream": np.concatenate([m_blocks(v["tw1"]), m_blocks(v["tw2"])]),
        "tables": v["emb_tables"].reshape(TABLES * VOCAB, D),
    }
    arrays = {k: np.ascontiguousarray(a) for k, a in arrays.items()}
    nc = bacc.Bacc("TRN2", target_bir_lowering=False, num_devices=1)
    t = {k: nc.dram_tensor(k, a.shape, mb.dt.from_np(a.dtype), kind="ExternalInput").ap() for k, a in arrays.items()}
    y = nc.dram_tensor("y", (1, BATCH), mb.dt.from_np(np.dtype("float32")), kind="ExternalOutput").ap()
    dlrm(nc, t["idx"], t["xt"], t["bw0"], t["bw1"], t["bw2"], t["bias"], t["w4"], t["b4"], t["wt0"], t["wt3"],
         t["wstream"], t["tables"], y)
    r = run_bass_kernel_spmd(nc, [arrays], core_ids=[0])
    return r.results[0]["y"].reshape(BATCH, 1)
```

```python
from contextlib import ExitStack

import concourse.bass as bass
from concourse import mybir

ALU = mybir.AluOpType
ACT = mybir.ActivationFunctionType
F32 = mybir.dt.float32
F32R = mybir.dt.float32r
I32 = mybir.dt.int32

P = 128
BATCH = 2048
TILE = 512
TILES = BATCH // TILE
SEG_UNITS = [2] * 8
SEGS = len(SEG_UNITS)
LOOP = (0, 6)
UNITS = BATCH // P
FIRST_UNIT = [sum(SEG_UNITS[:s]) for s in range(SEGS)]
WIDE = [P * n for n in SEG_UNITS]
BASE = [P * n for n in FIRST_UNIT]
TABLES = 26
VOCAB = 12500
D = 128
ITEMS = TABLES + 1
ITEM_PITCH = 32
PAIRS = ITEMS * (ITEMS - 1) // 2
TOP_IN = D + PAIRS + 1
DENSE = 13
S = 4
GRAM_M = (S - 1) * ITEM_PITCH + ITEMS
COLS = ITEMS - 1
GRAM_N = S * ITEM_PITCH

CHUNK = 4
CHUNKS = -(-TABLES // CHUNK)
WIDTH = [min(CHUNK, TABLES - CHUNK * k) for k in range(CHUNKS)]
GROUPS = 4
GRAMS = P // (S * GROUPS)
FWDS = -(-ITEMS // CHUNK)
PAIR_TILES = 3
PAIR_ROWS = [P, P, PAIRS + 1 - 2 * P]

BOT_SIZES = [512, 256, 128]
BOT_BLOCKS = 7
NB = TILES * BOT_BLOCKS
BOT_SPLIT = 6
L0, L1, L2, L3, L4 = 0, 8, 16, 20, 22
BLOCKS = 24
STREAM = 12
RAW_HEAD = 10
RAWC = 1024


def pair_at(n):
    return sum(ITEMS - 1 - i for i in range(n + 1, COLS))


def fwd_columns(f):
    top = ITEMS - CHUNK * f
    return range(max(0, top - CHUNK), top)


def unit_segment(U):
    return max(s for s in range(SEGS) if FIRST_UNIT[s] <= U)


def top_blocks(seg):
    return BLOCKS if WIDE[seg] == TILE else BLOCKS - 1



PAUSE = ("pause",)


def front_steps(seg):
    steps = []
    for U in range(FIRST_UNIT[seg], FIRST_UNIT[seg] + SEG_UNITS[seg]):
        steps += [("chunk", U, k) for k in range(CHUNKS)] + [PAUSE] + gram_steps(U)
    return steps[AHEAD if seg > 0 else 0:]


def ahead_steps(seg):
    return [("chunk", FIRST_UNIT[seg], k) for k in range(AHEAD)] if seg < SEGS else []


def gram_steps(U):
    return [("gram", U, h) for h in range(GRAMS)]


def fwd_steps(seg, a, b):
    return [("fwd", seg, f) for f in range(a, b)]


def back_steps(seg, a, b):
    return [("back", seg, k) for k in range(a, b)]


def halves(blocks):
    return [x for b in blocks for x in ([("part", *b[1:]), b] if L1 <= b[2] < L3 else [b])]


def weave(blocks, front, lead):
    slots = halves(blocks)
    steps, put = front[:lead], lead
    for i, b in enumerate(slots):
        steps.append(b)
        upto = lead + round((len(front) - lead) * (i + 1) / len(slots))
        steps += front[put:upto]
        put = upto
    return [st for st in steps if st != PAUSE]


def head_schedule():
    bottoms = [("bottom", 0, b) for b in range(4)]
    for t in range(TILES + 1):
        for b in ((t + 1, 0), (t + 1, 1), (t, 4), (t + 1, 2), (t + 1, 3), (t, 5), (t - 1, 6)):
            if 0 <= b[0] < TILES:
                bottoms.append(("bottom", *b))
    at = {("bottom", 0, 3): [("raw", 3), ("pads",)], ("bottom", 0, 4): [("raw", 4)]}
    rest = [("raw", r) for r in range(5, RAW_HEAD)]
    for r, i in zip(rest, HEAD_RAW):
        at.setdefault(bottoms[i], []).append(r)
    front = [st for st in front_steps(0) if st != PAUSE]
    steps = [("raw", r) for r in range(3)]
    for i, b in enumerate(bottoms):
        steps.append(b)
        steps += at.get(b, [])
        for _ in range(HEAD_FRONT.count(i)):
            steps.append(front.pop(0))
    steps += front + fwd_steps(0, 0, FWDS) + [("x0", 0)] + back_steps(0, 0, 2) + ahead_steps(1) + back_steps(0, 2, 3)
    return steps + [("split", 0, 0), ("split", 0, 1)]


HEAD_FRONT = [3, 5, 8, 11, 14, 16, 18, 20, 21, 22, 23, 23, 24, 24, 25, 25, 26, 26, 27]
HEAD_RAW = [8, 10, 13, 16, 19]


def segment_schedule(seg):
    b = [("block", seg, b) for b in range(top_blocks(seg))]
    n = seg + 1
    if n == SEGS:
        return with_splits(halves(b), seg, None)
    steps = weave(b[:18], front_steps(n), LEAD)
    steps += halves(b[18:19]) + fwd_steps(n, 0, 2)
    steps += halves(b[19:20])[:1] + fwd_steps(n, 2, 5) + b[19:20] + fwd_steps(n, 5, 7) + b[20:21]
    steps += [("x0", n)] + back_steps(n, 0, 1) + b[21:22] + back_steps(n, 1, 2)
    steps += ahead_steps(n + 1) + b[22:] + back_steps(n, 2, 3)
    return with_splits(steps, seg, n)


AHEAD = 1
LEAD = 0


def with_splits(steps, seg, nxt):
    out, due = [], []
    for st in steps:
        if st[0] in ("part", "block"):
            out += due
            due = []
        out.append(st)
        if st[0] == "block" and L1 <= st[2] < L3:
            k = st[2] - L1 + 2
            if k < STREAM:
                due = [("split", seg, k)]
    return out + ([("split", nxt, 0), ("split", nxt, 1)] if nxt else [])


SCHEDULE = [head_schedule()] + [segment_schedule(s) for s in range(SEGS)]


def emptied_by(step):
    return "A" if step[0] == "fwd" else "B"


def number_steps():
    tp_at, tp_a, tp_d, blk_at, split_at = {}, {}, {}, {}, {}
    a = d = 0
    for st in (st for part in SCHEDULE for st in part):
        if st[0] in ("chunk", "fwd", "back"):
            tp_at[st] = len(tp_at) + 1
            a += 1
            d += emptied_by(st) == "B"
            tp_a[tp_at[st]], tp_d[tp_at[st]] = a, d
        elif st[0] in ("bottom", "block"):
            blk_at[st] = len(blk_at) + 1
            if st[2] < (BOT_SPLIT if st[0] == "bottom" else L4):
                split_at[st] = len(split_at) + 1
    return tp_at, tp_a, tp_d, blk_at, split_at


TP_AT, TP_A, TP_D, BLK_AT, SPLIT_AT = number_steps()

_a, _b = ("fwd", LOOP[0] + 1, 0), ("fwd", LOOP[0] + 2, 0)
PER_TP = TP_AT[_b] - TP_AT[_a]
PER_A = TP_A[TP_AT[_b]] - TP_A[TP_AT[_a]]
PER_D = TP_D[TP_AT[_b]] - TP_D[TP_AT[_a]]
PER_UNITS = SEG_UNITS[LOOP[0]]
PER_BLK = top_blocks(LOOP[0])
PER_WIDE = WIDE[LOOP[0]]
PER_SPLIT = L4
PER_GP = GRAMS * PER_UNITS
assert not any(n % 2 for n in (PER_TP, PER_UNITS, PER_SPLIT, PER_GP, STREAM))


def raw_number(seg, k):
    return RAW_HEAD + STREAM * seg + k + 1


def dlrm(nc, idx, xt, bw0, bw1, bw2, bias, w4, b4, wt0, wt3, wstream, tables, y):
    with ExitStack() as ctx:
        def sb(name, shape, dt):
            return ctx.enter_context(nc.sbuf_tensor(name, shape, dt))

        def sem(name):
            return ctx.enter_context(nc.semaphore(name))

        W0 = sb("W0", [P, 2, 4, 1024], F32R)
        W3 = sb("W3", [P, 2, RAWC], F32R)
        W4 = sb("W4", [P, 2, 2], F32R)
        Wring = sb("Wring", [P, 2, 2, RAWC], F32R)
        raw = sb("raw", [P, 2, RAWC], F32)
        w4raw = sb("w4raw", [P, 2], F32)
        A = sb("A", [P, 16, TILE], F32R)
        B = sb("B", [P, 16, TILE], F32R)
        staged = sb("staged", [P, 2, TILE], F32)
        bottom_out = sb("bottom_out", [P, BATCH], F32)
        biases = sb("biases", [P, 29], F32)
        bias4 = sb("bias4", [1, 1], F32)
        G = sb("G", [P, TABLES * D], F32)
        E = sb("E", [P, 2, P, ITEM_PITCH], F32R)
        X = sb("X", [P, ITEMS, P], F32)
        Z = sb("Z", [P, S, PAIRS + 1], F32)
        ident = sb("ident", [P, P], F32)
        idx_all = sb("idx_all", [P, UNITS * TABLES], I32)
        idx_unit = sb("idx_unit", [P, 2, TABLES], I32)

        tp = ctx.enter_context(nc.psum_tensor("tp", [P, 2, 512], F32))
        gp = ctx.enter_context(nc.psum_tensor("gp", [P, 2, GROUPS, 2, GRAM_N], F32))
        mp = ctx.enter_context(nc.psum_tensor("mp", [P, 2, 512], F32))

        R = X[:, :, 0:S * ITEMS].rearrange("q n (s m) -> q n s m", s=S)
        XS = B[:, 8:12, :].rearrange("p a b -> p (a b)")
        BW0 = B[:, 12, :]

        idx_landed = sem("idx_landed")
        small_landed = sem("small_landed")
        raw_landed = [sem(f"raw_landed{i}") for i in range(2)]
        table_offsets = sem("table_offsets")
        consts = sem("consts")
        pads = sem("pads")
        idx_step = sem("idx_step")
        idx_ready = sem("idx_ready")
        idx_copied = sem("idx_copied")
        gather_turn = sem("gather_turn")
        bank_turn = sem("bank_turn")
        gathered = [sem(f"gathered{k}") for k in range(CHUNKS)]
        w_hi, w_lo, w4_ready = sem("w_hi"), sem("w_lo"), sem("w4_ready")
        w4_hi = sem("w4_hi")
        tp_done, tp_act, tp_dve = sem("tp_done"), sem("tp_act"), sem("tp_dve")
        item0_hi, item0_lo = sem("item0_hi"), sem("item0_lo")
        pairs_added = sem("pairs_added")
        gp_done, gp_act, gp_dve = sem("gp_done"), sem("gp_act"), sem("gp_dve")
        x0_hi, x0_lo = sem("x0_hi"), sem("x0_lo")
        block_done = sem("block_done")
        block_emptied, h_hi, h_lo = sem("block_emptied"), sem("h_hi"), sem("h_lo")
        y_stored = sem("y_stored")

        block = ctx.enter_context(nc.Block())

        def run(engine, step):
            for part in SCHEDULE[:LOOP[0] + 1]:
                for kind, *a in part:
                    step(None, kind, *a)
            with engine.Fori(0, LOOP[1] - LOOP[0]) as it:
                for kind, *a in SCHEDULE[LOOP[0] + 1]:
                    step(it, kind, *a)
            for part in SCHEDULE[LOOP[1] + 1:]:
                for kind, *a in part:
                    step(None, kind, *a)

        def at(it, n, per):
            return n if it is None else n + it * per

        @block.sync
        def _(sp):
            sp.dma_start(idx_all[:], idx).then_inc(idx_landed, 16)
            loads = [(raw[0:96, 0, 0:512], bw0), (raw[0:96, 1, :], xt[0]),
                     (raw[:, 0, :], bw1), (raw[:, 1, 0:256], bw2), (raw[0:96, 0, :], xt[1])]
            loads += [(raw[:, (5 + k) % 2, :], wt0[:, k, :]) for k in range(4)]
            loads += [(raw[:, 1, :], wt3)]
            for r, (dst, src) in enumerate(loads):
                if r >= 2:
                    sp.wait_ge(w_lo, r - 1)
                sp.dma_start(dst, src).then_inc(raw_landed[r % 2], 16)
                if r == 1:
                    sp.dma_start(biases[:], bias).then_inc(small_landed, 16)
                    sp.dma_start(w4raw[:], w4).then_inc(small_landed, 16)
                    sp.dma_start(bias4[:], b4).then_inc(small_landed, 16)
            for k in range(2):
                sp.wait_ge(w_lo, raw_number(0, k) - 2)
                sp.dma_start(raw[:, k, :], wstream[k]).then_inc(raw_landed[k], 16)

            def reload(seg, k):
                sp.wait_ge(w_lo, seg * STREAM + raw_number(0, k))
                sp.dma_start(raw[:, k % 2, :], wstream[(k + 2) % STREAM]).then_inc(raw_landed[k % 2], 16)

            with sp.Fori(0, SEGS - 1) as seg:
                for k in range(STREAM):
                    reload(seg, k)
            for k in range(STREAM - 2):
                reload(SEGS - 1, k)
            sp.wait_ge(block_emptied, len(BLK_AT))
            sp.dma_start(y, bottom_out[0:1, :]).then_inc(y_stored, 16)
            sp.wait_ge(y_stored, 16)

        @block.gpsimd
        def _(pool):
            offs = X[:, 0:4, :].rearrange("p a b -> p (a b)").bitcast(I32)[:, 0:UNITS * TABLES]
            pool.iota(offs.rearrange("p (a t) -> p a t", t=TABLES), pattern=[[0, UNITS], [VOCAB, TABLES]],
                      base=0, channel_multiplier=0).then_inc(table_offsets, 1)
            pool.memset(ident[:], 0.0).then_inc(consts, 1)
            pool.wait_ge(consts, 1)
            pool.affine_select(out=ident[:], in_=ident[:], compare_op=ALU.not_equal, fill=1.0, base=0,
                               pattern=[[-1, P]], channel_multiplier=1).then_inc(consts, 1)
            pool.wait_ge(idx_ready, 1)

            def copy_indices(U, par):
                pool.tensor_copy(idx_unit[:, par, :], idx_all[:, bass.ds(U * TABLES, TABLES)]).then_inc(idx_copied, 1)
                pool.wait_ge(idx_copied, U + 1)
                pool.sem_inc(gather_turn, 1)

            def gather_unit(U, it=None):
                for k in range(CHUNKS):
                    if U > 0:
                        pool.wait_ge(tp_done, at(it, TP_AT["chunk", U - 1, k], PER_TP))
                    if k == 0:
                        copy_indices(at(it, U, PER_UNITS), U % 2)
                    else:
                        pool.sem_inc(gather_turn, 1)
                    for i in range(WIDTH[k]):
                        t = CHUNK * k + i
                        pool.indirect_dma_start(G[:, t * D:(t + 1) * D], None, tables,
                                                bass.IndirectOffsetOnAxis(idx_unit[:, U % 2, t:t + 1], 0)
                                                ).then_inc(gathered[k], 16)

            first = FIRST_UNIT[LOOP[0] + 1] + 1
            turns = min(LOOP[1] - LOOP[0], (UNITS - first) // PER_UNITS)
            for U in range(first):
                gather_unit(U)
            with pool.Fori(0, turns) as it:
                for U in range(first, first + PER_UNITS):
                    gather_unit(U, it)
            for U in range(first + PER_UNITS * turns, UNITS):
                gather_unit(U)

        def segment_out(seg, it):
            return bottom_out[:, bass.ds(at(it, BASE[seg], PER_WIDE), WIDE[seg])]

        def mp_bank(st):
            if st[0] == "bottom":
                return (BLK_AT[st] - 1) % 2
            return 1 if st[2] == top_blocks(st[1]) - 1 else st[2] % 2

        def item0_source(U, it):
            seg = unit_segment(U)
            src = segment_out(seg, it).rearrange("d (s j g) -> d j g s", s=S, j=SEG_UNITS[seg])
            return src[:, U - FIRST_UNIT[seg]]

        def item0_views(U, it):
            return (*(E[:, h, :, 0].rearrange("d (g s) -> d g s", s=S) for h in range(2)), item0_source(U, it))

        def gram_views(s, U, h):
            rows = ITEM_PITCH if s < S - 1 else ITEMS
            q = P // S * (U - FIRST_UNIT[unit_segment(U)]) + GROUPS * h
            at_s = slice(s * ITEM_PITCH, s * ITEM_PITCH + ITEMS)
            u, v = (gp[32 * s:32 * s + rows, h % 2, :, i, at_s] for i in range(2))
            return X[32 * s:32 * s + rows, :, q:q + GROUPS].rearrange("p n i -> p i n"), u, v

        def tp_bank(st):
            return (TP_AT[st] - 1) % 2

        def chunk_views(U, k):
            hi, lo = (E[:, h, :, 1 + CHUNK * k:1 + CHUNK * k + WIDTH[k]].rearrange("d p i -> d i p") for h in range(2))
            src = tp[:, tp_bank(("chunk", U, k)), 0:WIDTH[k] * P]
            return hi, lo, src.rearrange("d (i p) -> d i p", i=WIDTH[k])

        def out_tiles(b):
            if b < L1:
                return A[:, b], A[:, 8 + b], 7 + b
            if b < L2:
                return B[:, b - L1], B[:, 8 + b - L1], 7 + b
            if b < L3:
                return A[:, b - L2], A[:, 4 + b - L2], 7 + b
            return B[:, 8 + b - L3], B[:, 10 + b - L3], 7 + b

        def bottom_tiles(t, b):
            if b < 4:
                return A[:, 8 * (t % 2) + b], A[:, 8 * (t % 2) + 4 + b], b
            return B[:, 4 * (t % 2) + b - 4], B[:, 4 * (t % 2) + b - 2], b

        def raw_parts(r):
            if r == 0:
                return raw[0:96, 0, 0:512], BW0[0:96], BW0, (32, 64)
            if r in (1, 4):
                half = XS[:, RAWC * (r // 4):RAWC * (r // 4 + 1)]
                return raw[0:96, r % 2, :], half[0:96], half, (64, 96)
            if r == 2:
                return raw[:, 0, :], Wring[:, 0, 0, :], Wring[:, 0, 1, :], (0, P)
            if r == 3:
                return raw[:, 1, 0:256], Wring[:, 1, 0, 0:256], Wring[:, 1, 1, 0:256], (0, P)
            if r < 9:
                return raw[:, r % 2, :], W0[:, 0, r - 5], W0[:, 1, r - 5], (0, P)
            return raw[:, 1, :], W3[:, 0], W3[:, 1], (0, P)

        def slot_used(seg, k):
            if seg == 0 and k < 2:
                return NB
            return BLK_AT["block", seg, L1 + k - 2] if k >= 2 else BLK_AT["block", seg - 1, L3 + k - 2]

        @block.scalar
        def _(act):
            def empty_split(it, st, col, w):
                n, ns = BLK_AT[st], SPLIT_AT[st]
                if ns > 2:
                    act.wait_ge(h_lo, at(it, ns - 2, PER_SPLIT))
                act.wait_ge(block_done, at(it, n, PER_BLK))
                act.activation(staged[:, (ns - 1) % 2, 0:w], mp[:, mp_bank(st), 0:w], ACT.Relu,
                               bias=biases[:, col:col + 1]).then_inc(block_emptied, 1)

            def step(it, kind, *a):
                st = (kind, *a)
                if kind == "raw":
                    r, = a
                    act.wait_ge(raw_landed[r % 2], 16 * (r // 2 + 1))
                    src, hi, _, _ = raw_parts(r)
                    act.activation(hi, src, ACT.Copy).then_inc(w_hi, 1)
                    if r == 3:
                        act.activation(W4[:, 0], w4raw[:], ACT.Copy).then_inc(w4_hi, 1)
                elif kind == "split":
                    seg, k = a
                    act.wait_ge(raw_landed[k % 2], at(it, 16 * ((raw_number(seg, k) - 1) // 2 + 1), 16 * STREAM // 2))
                    act.wait_ge(block_done, at(it, slot_used(seg, k), PER_BLK))
                    act.activation(Wring[:, k % 2, 0], raw[:, k % 2], ACT.Copy).then_inc(w_hi, 1)
                elif kind == "bottom":
                    t, b = a
                    if b < BOT_SPLIT:
                        empty_split(None, st, bottom_tiles(t, b)[2], TILE)
                    else:
                        act.wait_ge(block_done, BLK_AT[st])
                        act.activation(bottom_out[:, t * TILE:(t + 1) * TILE], mp[:, mp_bank(st), :], ACT.Relu,
                                       bias=biases[:, 6:7]).then_inc(block_emptied, 1)
                elif kind == "block":
                    seg, b = a
                    if b < L4:
                        empty_split(it, st, out_tiles(b)[2], WIDE[seg])
                    else:
                        act.wait_ge(block_done, at(it, BLK_AT[st], PER_BLK))
                        act.activation(bottom_out[0:1, bass.ds(at(it, BASE[seg] + (b - L4) * 256, PER_WIDE), 256)],
                                       mp[0:1, mp_bank(st), 0:256], ACT.Identity, bias=bias4[:]
                                       ).then_inc(block_emptied, 1)
                elif kind == "chunk":
                    U, k = a
                    if k == 0 and U > 0:
                        act.wait_ge(gp_done, at(it, GRAMS * U, PER_GP))
                    if k == CHUNKS - 1:
                        tile = BASE[unit_segment(U)] // TILE
                        act.wait_ge(block_emptied, BLK_AT["bottom", tile if it is None else TILES - 1, 6])
                        hi, _, src = item0_views(U, it)
                        act.activation(hi, src, ACT.Copy).then_inc(item0_hi, 1)
                    act.wait_ge(tp_done, at(it, TP_AT[st], PER_TP))
                    hi, _, src = chunk_views(U, k)
                    act.activation(hi, src, ACT.Copy).then_inc(tp_act, 1)
                elif kind == "gram":
                    U, h = a
                    seg = unit_segment(U)
                    if seg > 0 and U == FIRST_UNIT[seg] and h == 0:
                        act.wait_ge(pairs_added, at(it, FWDS * seg, FWDS))
                    act.wait_ge(gp_done, at(it, GRAMS * U + h + 1, PER_GP))
                    for s in range(S):
                        dst, u, _ = gram_views(s, U, h)
                        half_u = act.activation(dst, u, ACT.Copy, scale=0.5)
                        if s % 2:
                            half_u.then_inc(gp_act, 1)
                elif kind == "fwd":
                    seg, f = a
                    act.wait_ge(tp_done, at(it, TP_AT[st], PER_TP))
                    rows, cols = WIDE[seg] // S, fwd_columns(f)
                    src = tp[0:rows, tp_bank(st), 0:len(cols) * P].rearrange("q (n s m) -> q n s m", s=S, m=ITEM_PITCH)
                    act.activation(R[0:rows, cols[0]:cols[-1] + 1], src[:, :, :, 0:ITEMS], ACT.Copy).then_inc(tp_act, 1)
                elif kind == "back":
                    seg, k = a
                    act.wait_ge(tp_done, at(it, TP_AT[st], PER_TP))
                    act.activation(B[0:PAIR_ROWS[k], 1 + k, 0:WIDE[seg]], tp[0:PAIR_ROWS[k], tp_bank(st), 0:WIDE[seg]],
                                   ACT.Copy).then_inc(tp_act, 1)
                elif kind == "x0":
                    seg, = a
                    act.activation(B[:, 0, 0:WIDE[seg]], segment_out(seg, it), ACT.Copy).then_inc(x0_hi, 1)

            act.wait_ge(small_landed, 48)
            run(act, step)

        @block.vector
        def _(dve):
            def minus_hi(dst, full, hi):
                return dve.tensor_tensor(dst, full, hi.bitcast(F32), ALU.subtract)

            def split_output(it, st, hi, lo, w):
                n = SPLIT_AT[st]
                whole = staged[:, (n - 1) % 2, 0:w]
                dve.wait_ge(block_emptied, at(it, BLK_AT[st], PER_BLK))
                dve.tensor_copy(hi[:, 0:w], whole).then_inc(h_hi, 1)
                dve.wait_ge(h_hi, at(it, n, PER_SPLIT))
                minus_hi(lo[:, 0:w], whole, hi[:, 0:w]).then_inc(h_lo, 1)

            def step(it, kind, *a):
                st = (kind, *a)
                if kind == "raw":
                    r, = a
                    dve.wait_ge(w_hi, r + 1)
                    src, hi, lo, (p0, p1) = raw_parts(r)
                    minus_hi(lo[p0:p1], src[p0:p1], hi[p0:p1]).then_inc(w_lo, 1)
                    if r == 3:
                        dve.wait_ge(w4_hi, 1)
                        minus_hi(W4[:, 1], w4raw[:], W4[:, 0]).then_inc(w4_ready, 1)
                elif kind == "pads":
                    dve.memset(E[:, :, :, ITEMS:ITEM_PITCH].bitcast(F32), 0.0).then_inc(pads, 1)
                    dve.memset(Z[:, :, PAIRS:PAIRS + 1], 0.0).then_inc(pads, 1)
                elif kind == "split":
                    seg, k = a
                    dve.wait_ge(w_hi, at(it, raw_number(seg, k), STREAM))
                    minus_hi(Wring[:, k % 2, 1], raw[:, k % 2], Wring[:, k % 2, 0]).then_inc(w_lo, 1)
                elif kind == "bottom":
                    t, b = a
                    if b < BOT_SPLIT:
                        hi, lo, _ = bottom_tiles(t, b)
                        split_output(None, st, hi, lo, TILE)
                elif kind == "block":
                    seg, b = a
                    if b < L4:
                        hi, lo, _ = out_tiles(b)
                        split_output(it, st, hi, lo, WIDE[seg])
                elif kind == "chunk":
                    U, k = a
                    if k == CHUNKS - 1:
                        dve.wait_ge(item0_hi, at(it, U + 1, PER_UNITS))
                        hi, lo, src = item0_views(U, it)
                        minus_hi(lo, src, hi).then_inc(item0_lo, 1)
                    dve.wait_ge(tp_act, at(it, TP_A[TP_AT[st]], PER_A))
                    hi, lo, src = chunk_views(U, k)
                    minus_hi(lo, src, hi).then_inc(tp_dve, 1)
                elif kind == "gram":
                    U, h = a
                    for s in range(S):
                        if s % 2 == 0:
                            dve.wait_ge(gp_act, at(it, 2 * (GRAMS * U + h) + 1 + s // 2, 2 * PER_GP))
                        dst, _, v = gram_views(s, U, h)
                        last = dve.tensor_tensor(dst, v, dst, ALU.add)
                    last.then_inc(gp_dve, 1)
                elif kind == "fwd":
                    seg, f = a
                    dve.wait_ge(tp_act, at(it, TP_A[TP_AT[st]], PER_A))
                    rows = WIDE[seg] // S
                    for n in fwd_columns(f):
                        if n < COLS:
                            last = dve.tensor_tensor(Z[0:rows, :, pair_at(n):pair_at(n) + COLS - n],
                                                     R[0:rows, n, :, n + 1:ITEMS],
                                                     R[0:rows, n + 1:ITEMS, :, n].rearrange("q m s -> q s m"), ALU.add)
                    last.then_inc(pairs_added, 1)
                elif kind == "back":
                    seg, k = a
                    dve.wait_ge(tp_act, at(it, TP_A[TP_AT[st]], PER_A))
                    minus_hi(B[0:PAIR_ROWS[k], 5 + k, 0:WIDE[seg]], tp[0:PAIR_ROWS[k], tp_bank(st), 0:WIDE[seg]],
                             B[0:PAIR_ROWS[k], 1 + k, 0:WIDE[seg]]).then_inc(tp_dve, 1)
                elif kind == "x0":
                    seg, = a
                    dve.wait_ge(x0_hi, at(it, seg + 1, 1))
                    minus_hi(B[:, 4, 0:WIDE[seg]], segment_out(seg, it), B[:, 0, 0:WIDE[seg]]).then_inc(x0_lo, 1)

            n_idx = UNITS * TABLES
            scratch = X[:].rearrange("p a b -> p (a b)")
            offs = scratch[:, 0:n_idx].bitcast(I32)
            wrap, clamped = scratch[:, 512:512 + n_idx], scratch[:, 1024:1024 + n_idx]
            dve.wait_ge(idx_landed, 16)
            dve.tensor_scalar(wrap, idx_all[:], 0.0, float(VOCAB), ALU.is_lt, ALU.mult).then_inc(idx_step, 1)
            dve.wait_ge(idx_step, 1)
            dve.tensor_tensor(clamped, wrap, idx_all[:], ALU.add).then_inc(idx_step, 1)
            dve.wait_ge(idx_step, 2)
            dve.tensor_scalar(clamped, clamped, 0.0, float(VOCAB - 1), ALU.max, ALU.min).then_inc(idx_step, 1)
            dve.wait_ge(idx_step, 3)
            dve.wait_ge(table_offsets, 1)
            dve.tensor_tensor(idx_all[:], clamped, offs, ALU.add).then_inc(idx_ready, 1)
            dve.wait_ge(small_landed, 48)
            run(dve, step)

        @block.tensor
        def _(pe):
            def products(st, k_tiles, width=TILE, half=None):
                out = mp[:, mp_bank(st), 0:width]
                last_k = len(k_tiles) - 1
                for k, (whi, wlo, xhi, xlo, wait) in enumerate(k_tiles):
                    if half is not None and k * 2 // len(k_tiles) != half:
                        continue
                    if wait:
                        pe.wait_ge(*wait)
                    o = out[0:whi.shape[1]]
                    pe.matmul(o, whi, xhi, start=(k == 0), stop=False)
                    pe.matmul(o, whi, xlo, start=False, stop=False)
                    last = pe.matmul(o, wlo, xhi, start=False, stop=(k == last_k))
                if half != 0:
                    last.then_inc(block_done, 1)

            def wait_for_bank(it, st):
                last = TP_AT[st] - 2
                if last < 1:
                    return
                if next(emptied_by(x) for x, n in TP_AT.items() if n == last) == "A":
                    pe.wait_ge(tp_act, at(it, TP_A[last], PER_A))
                else:
                    pe.wait_ge(tp_dve, at(it, TP_D[last], PER_D))
                if st[0] != "chunk":
                    pe.sem_inc(bank_turn, 1)

            def step(it, kind, *a):
                st = (kind, *a)
                halved = kind == "part" or kind == "block" and L1 <= a[1] < L3
                if kind in ("bottom", "block") and BLK_AT[st] > 2 and not halved:
                    back = 1 if kind == "block" and a[1] == top_blocks(a[0]) - 1 and a[1] % 2 == 0 else 2
                    pe.wait_ge(block_emptied, at(it, BLK_AT[st] - back, PER_BLK))
                if kind == "bottom":
                    t, b = a
                    if b < 4:
                        pe.wait_ge(w_lo, 2 if t < 2 else 5)
                        pe.matmul(mp[:, mp_bank(st), :], BW0[0:96, b * P:(b + 1) * P],
                                  XS[0:96, t * TILE:(t + 1) * TILE], start=True, stop=True).then_inc(block_done, 1)
                    elif b < 6:
                        m = b - 4
                        pe.wait_ge(w_lo, 3)
                        products(st, [(Wring[:, 0, 0, k * 256 + m * P:k * 256 + (m + 1) * P],
                                       Wring[:, 0, 1, k * 256 + m * P:k * 256 + (m + 1) * P],
                                       *bottom_tiles(t, k)[:2], (h_lo, SPLIT_AT["bottom", t, k])) for k in range(4)])
                    else:
                        pe.wait_ge(w_lo, 4)
                        products(st, [(Wring[:, 1, 0, k * P:(k + 1) * P], Wring[:, 1, 1, k * P:(k + 1) * P],
                                       *bottom_tiles(t, 4 + k)[:2], (h_lo, SPLIT_AT["bottom", t, 4 + k]))
                                      for k in range(2)])
                elif kind in ("part", "block"):
                    seg, b = a
                    w = WIDE[seg]

                    def ready(first, k):
                        return (h_lo, at(it, SPLIT_AT["block", seg, first + k], PER_SPLIT))

                    if b < L1:
                        if b == 0:
                            pe.wait_ge(w_lo, RAW_HEAD)
                        x_ready = [(x0_lo, at(it, seg + 1, 1))]
                        x_ready += [(tp_dve, at(it, TP_D[TP_AT["back", seg, k]], PER_D)) for k in range(PAIR_TILES)]
                        rows = [P] + PAIR_ROWS
                        products(st, [(W0[0:rows[k], 0, k, b * P:(b + 1) * P], W0[0:rows[k], 1, k, b * P:(b + 1) * P],
                                       B[0:rows[k], k, 0:w], B[0:rows[k], 4 + k, 0:w], x_ready[k] if b == 0 else None)
                                      for k in range(4)], w)
                    elif b < L3:
                        q, blk = b - L1, ("block", seg, b)
                        if kind == "part":
                            pe.wait_ge(block_emptied, at(it, BLK_AT[blk] - 2, PER_BLK))
                            pe.wait_ge(w_lo, at(it, raw_number(seg, q), STREAM))
                        src, first = (A, L0) if b < L2 else (B, L1)
                        start = b in (L1, L2)
                        products(blk, [(Wring[:, q % 2, 0, k * P:(k + 1) * P], Wring[:, q % 2, 1, k * P:(k + 1) * P],
                                        src[:, k, 0:w], src[:, 8 + k, 0:w], ready(first, k) if start else None)
                                       for k in range(8)], w, half=0 if kind == "part" else 1)
                    elif b < L4:
                        m = b - L3
                        products(st, [(W3[:, 0, k * 256 + m * P:k * 256 + (m + 1) * P],
                                       W3[:, 1, k * 256 + m * P:k * 256 + (m + 1) * P],
                                       A[:, k, 0:w], A[:, 4 + k, 0:w], ready(L2, k) if m == 0 else None)
                                      for k in range(4)], w)
                    else:
                        if seg == 0:
                            pe.wait_ge(w4_ready, 1)
                        c = slice((b - L4) * 256, (b - L4 + 1) * 256)
                        products(st, [(W4[:, 0, k:k + 1], W4[:, 1, k:k + 1], B[:, 8 + k, c], B[:, 10 + k, c],
                                       ready(L3, k) if b == L4 else None) for k in range(2)], 256)
                elif kind == "chunk":
                    U, k = a
                    pe.wait_ge(gathered[k], at(it, 16 * WIDTH[k] * (U + 1), 16 * WIDTH[k] * PER_UNITS))
                    wait_for_bank(it, st)
                    for i in range(WIDTH[k]):
                        t = CHUNK * k + i
                        last = pe.transpose(tp[:, tp_bank(st), i * P:(i + 1) * P], G[:, t * D:(t + 1) * D], ident[:])
                    last.then_inc(tp_done, 1)
                elif kind == "gram":
                    U, h = a
                    if U == 0 and h == 0:
                        pe.wait_ge(pads, 2)
                        pe.wait_ge(idx_ready, 1)
                    if h == 0:
                        pe.wait_ge(tp_dve, at(it, TP_D[TP_AT["chunk", U, CHUNKS - 1]], PER_D))
                        pe.wait_ge(item0_lo, at(it, U + 1, PER_UNITS))
                    if GRAMS * U + h >= 2:
                        pe.wait_ge(gp_dve, at(it, GRAMS * U + h - 1, PER_GP))
                    for i in range(GROUPS):
                        p = S * (GROUPS * h + i)
                        last = pe.matmul(gp[0:GRAM_M, h % 2, i].rearrange("p h n -> p (h n)"),
                                         E[:, 0, p:p + S, :].rearrange("d s m -> d (s m)")[:, 0:GRAM_M],
                                         E[:, :, p:p + S, :].rearrange("d h s m -> d h (s m)"),
                                         start=True, stop=True)
                    last.then_inc(gp_done, 1)
                elif kind == "fwd":
                    seg, f = a
                    if f == 0:
                        pe.wait_ge(gp_dve, at(it, GRAMS * (FIRST_UNIT[seg] + SEG_UNITS[seg]), PER_GP))
                    wait_for_bank(it, st)
                    rows = WIDE[seg] // S
                    for i, n in enumerate(fwd_columns(f)):
                        last = pe.transpose(tp[0:rows, tp_bank(st), i * P:i * P + GRAM_M], X[0:GRAM_M, n, 0:rows],
                                            ident[0:GRAM_M, 0:GRAM_M])
                    last.then_inc(tp_done, 1)
                elif kind == "back":
                    seg, k = a
                    f = max(f for f in range(FWDS) for n in fwd_columns(f) if n < COLS and pair_at(n) < P * (k + 1))
                    pe.wait_ge(pairs_added, at(it, FWDS * seg + f + 1, FWDS))
                    wait_for_bank(it, st)
                    rows = WIDE[seg] // S
                    for s in range(S):
                        last = pe.transpose(tp[0:PAIR_ROWS[k], tp_bank(st), s * rows:(s + 1) * rows],
                                            Z[0:rows, s, k * P:k * P + PAIR_ROWS[k]], ident[0:rows, 0:rows])
                    last.then_inc(tp_done, 1)

            pe.wait_ge(consts, 2)
            run(pe, step)


def kernel(**inputs):
    import numpy as np
    import concourse.bacc as bacc
    from concourse import mybir as mb
    from concourse.bass_utils import run_bass_kernel_spmd

    v = {k.replace("L0_rec_", ""): np.asarray(a) for k, a in inputs.items()}
    idx = [v["r_categorical_inputs"][b:b + w].reshape(S, n, P // S, TABLES).transpose(2, 0, 1, 3).reshape(P, -1)
           for b, w, n in zip(BASE, WIDE, SEG_UNITS)]
    xt3 = np.zeros((96, BATCH), np.float32)
    bw03 = np.zeros((96, BOT_SIZES[0]), np.float32)
    for q in range(3):
        xt3[32 * q:32 * q + DENSE] = v["r_numerical_input"].T
        bw03[32 * q:32 * q + DENSE] = v["bw0"].T

    def k_major(w):
        out, k = w.shape
        return w.T.reshape(k // P, P, out).transpose(1, 0, 2)

    def m_blocks(w):
        out, k = w.shape
        return w.reshape(out // P, P, k // P, P).transpose(0, 3, 2, 1).reshape(out // P, P, k)

    order = [D + m * (m - 1) // 2 + n for n in reversed(range(COLS)) for m in range(n + 1, ITEMS)]
    cols = list(range(D)) + order + [TOP_IN - 1]
    w0 = np.zeros((1024, 4 * P), np.float32)
    w0[:, :TOP_IN] = v["tw0"][:, cols]
    bias = np.concatenate([v[n].reshape(-1, P) for n in ("bb0", "bb1", "bb2", "tb0", "tb1", "tb2", "tb3")]).T
    arrays = {
        "idx": np.concatenate(idx, axis=1),
        "xt": np.stack([xt3[:, :RAWC], xt3[:, RAWC:]]),
        "bw0": bw03,
        "bw1": k_major(v["bw1"]).reshape(P, -1),
        "bw2": k_major(v["bw2"]).reshape(P, -1),
        "bias": bias,
        "w4": v["tw4"].reshape(2, P).T,
        "b4": v["tb4"].reshape(1, 1),
        "wt0": k_major(w0),
        "wt3": k_major(v["tw3"]).reshape(P, -1),
        "wstream": np.concatenate([m_blocks(v["tw1"]), m_blocks(v["tw2"])]),
        "tables": v["emb_tables"].reshape(TABLES * VOCAB, D),
    }
    arrays = {k: np.ascontiguousarray(a) for k, a in arrays.items()}
    nc = bacc.Bacc("TRN2", target_bir_lowering=False, num_devices=1)
    t = {k: nc.dram_tensor(k, a.shape, mb.dt.from_np(a.dtype), kind="ExternalInput").ap() for k, a in arrays.items()}
    y = nc.dram_tensor("y", (1, BATCH), mb.dt.from_np(np.dtype("float32")), kind="ExternalOutput").ap()
    dlrm(nc, t["idx"], t["xt"], t["bw0"], t["bw1"], t["bw2"], t["bias"], t["w4"], t["b4"], t["wt0"], t["wt3"],
         t["wstream"], t["tables"], y)
    r = run_bass_kernel_spmd(nc, [arrays], core_ids=[0])
    return r.results[0]["y"].reshape(BATCH, 1)
```
